# Optimizing a Trainium2 kernel written in Bass

```python
import numpy as np
import jax
import jax.numpy as jnp

def _softmax(x, axis=-1):
    return jax.nn.softmax(x, axis=axis)

def _gelu(x):
    return jax.nn.gelu(x, approximate=True)

def _silu(x):
    return jax.nn.silu(x)

def _sigmoid(x):
    return jax.nn.sigmoid(x)

def _layernorm(x, axis=-1, eps=1e-05):
    m = jnp.mean(x, axis=axis, keepdims=True)
    v = jnp.var(x, axis=axis, keepdims=True)
    return (x - m) / jnp.sqrt(v + eps)

def _scatter_add(tgt, idx, src, axis=0):
    return tgt.at[idx].add(src)

def _segment_sum(src, seg, n):
    return jax.ops.segment_sum(src, seg, n)
kernel_name = 'mk_xattn_seq_d4_seqx_r4_5462b0'

def setup_inputs(seed: int=0):
    np.random.seed(seed)
    _w = jnp.asarray

    def _rec_inputs():
        import jax
        import jax.numpy as jnp
        _rk = jax.random.key(seed)
        x = -0.0003929 + 0.9999 * jax.random.normal(jax.random.fold_in(_rk, 1), (64, 128, 256), jnp.float32)
        _lenS = 128 - jax.random.randint(jax.random.fold_in(_rk, 7), (64,), 0, max(1, 128 // 4) + 1, jnp.int32)
        _lenS2 = 128 - jax.random.randint(jax.random.fold_in(_rk, 8), (64,), 0, max(1, 128 // 4) + 1, jnp.int32)
        _ctx_512P = jax.random.normal(jax.random.fold_in(_rk, 11), (64, 16, 128), jnp.float32)
        _ctx_512c = jax.random.dirichlet(jax.random.fold_in(_rk, 511), 0.3 * jnp.ones((16,), jnp.float32), (64, 128))
        _ctx_512t = jnp.einsum('bsk,bkd->bsd', _ctx_512c, _ctx_512P)
        _ctx_512t = _ctx_512t * jax.lax.rsqrt(jnp.mean(jnp.square(_ctx_512t)) + 1e-12) * 0.953939
        ctx_512 = 4.13588e-05 + 0.999923 * (_ctx_512t + 0.3 * jax.random.normal(jax.random.fold_in(_rk, 611), (64, 128, 128), jnp.float32))
        fside_BxSxS_0 = 0.000376506 + 0.999991 * jax.random.normal(jax.random.fold_in(_rk, 12), (64, 128, 128), jnp.float32)
        return (x, ctx_512, fside_BxSxS_0)
    x, ctx_512, fside_BxSxS_0 = _rec_inputs()

    def _L0_xattn_setup():
        import jax, jax.numpy as jnp
        import numpy as np
        QUERY_DIM = 256
        KEY_DIM = 128
        HIDDEN_DIM = 256
        B, LQ, LK = (8, 512, 512)
        key = jax.random.key(seed)
        ks = jax.random.split(key, 10)
        s_q = 1.0 / np.sqrt(QUERY_DIM)
        s_k = 1.0 / np.sqrt(KEY_DIM)
        s_h = 1.0 / np.sqrt(HIDDEN_DIM)
        return {'query': jax.random.normal(ks[0], (B, LQ, QUERY_DIM), jnp.float32), 'key': jax.random.normal(ks[1], (B, LK, KEY_DIM), jnp.float32), 'Wq': jax.random.uniform(ks[2], (QUERY_DIM, HIDDEN_DIM), jnp.float32, -s_q, s_q), 'bq': jax.random.uniform(ks[3], (HIDDEN_DIM,), jnp.float32, -s_q, s_q), 'Wk': jax.random.uniform(ks[4], (KEY_DIM, HIDDEN_DIM), jnp.float32, -s_k, s_k), 'bk': jax.random.uniform(ks[5], (HIDDEN_DIM,), jnp.float32, -s_k, s_k), 'Wv': jax.random.uniform(ks[6], (KEY_DIM, HIDDEN_DIM), jnp.float32, -s_k, s_k), 'bv': jax.random.uniform(ks[7], (HIDDEN_DIM,), jnp.float32, -s_k, s_k), 'Wo': jax.random.uniform(ks[8], (HIDDEN_DIM, QUERY_DIM), jnp.float32, -s_h, s_h), 'bo': jax.random.uniform(ks[9], (QUERY_DIM,), jnp.float32, -s_h, s_h)}
    _L0_xattn_all = _L0_xattn_setup()
    _L0_xattn_in = {k: v for k, v in _L0_xattn_all.items() if k in ('Wq', 'bq', 'Wk', 'bk', 'Wv', 'bv', 'Wo', 'bo')}
    del _L0_xattn_all

    def _L1_xattn_setup():
        import jax, jax.numpy as jnp
        import numpy as np
        EPS = 1e-05

        def _ln(x, g, b):
            mu = jnp.mean(x, axis=-1, keepdims=True)
            var = jnp.var(x, axis=-1, keepdims=True)
            return (x - mu) * jax.lax.rsqrt(var + EPS) * g + b

        def _cma(x1, x2, ln1_g, ln1_b, ln2_g, ln2_b, Wq, bq, Wk, bk, Wv, bv, Wo, bo):
            e = Wq.shape[1]
            scale = e ** (-0.5)
            x1n = _ln(x1, ln1_g, ln1_b)
            x2n = _ln(x2, ln2_g, ln2_b)
            q = x1n @ Wq + bq
            k = x2n @ Wk + bk
            v = x2n @ Wv + bv
            attn = jax.nn.softmax(jnp.einsum('bqe,bke->bqk', q, k) * scale, axis=-1)
            ctx = jnp.einsum('bqk,bke->bqe', attn, v)
            return ctx @ Wo + bo
        key = jax.random.key(seed)
        ks = jax.random.split(key, 24)
        B, Lt, La, Lv = (16, 128, 256, 128)
        Dt, Da, Dv, E = (256, 128, 128, 256)
        s = lambda k, *sh: jax.random.normal(k, sh, dtype=jnp.float32) * 0.02
        inp = {'text': jax.random.normal(ks[0], (B, Lt, Dt), dtype=jnp.float32), 'audio': jax.random.normal(ks[1], (B, La, Da), dtype=jnp.float32), 'video': jax.random.normal(ks[2], (B, Lv, Dv), dtype=jnp.float32), 'a_ln1_g': jnp.ones((Dt,)), 'a_ln1_b': jnp.zeros((Dt,)), 'a_ln2_g': jnp.ones((Da,)), 'a_ln2_b': jnp.zeros((Da,)), 'a_Wq': s(ks[3], Dt, E), 'a_bq': jnp.zeros((E,)), 'a_Wk': s(ks[4], Da, E), 'a_bk': jnp.zeros((E,)), 'a_Wv': s(ks[5], Da, E), 'a_bv': jnp.zeros((E,)), 'a_Wo': s(ks[6], E, Dt), 'a_bo': jnp.zeros((Dt,)), 'v_ln1_g': jnp.ones((Dt,)), 'v_ln1_b': jnp.zeros((Dt,)), 'v_ln2_g': jnp.ones((Dv,)), 'v_ln2_b': jnp.zeros((Dv,)), 'v_Wq': s(ks[7], Dt, E), 'v_bq': jnp.zeros((E,)), 'v_Wk': s(ks[8], Dv, E), 'v_bk': jnp.zeros((E,)), 'v_Wv': s(ks[9], Dv, E), 'v_bv': jnp.zeros((E,)), 'v_Wo': s(ks[10], E, Dt), 'v_bo': jnp.zeros((Dt,)), 'ln_g': jnp.ones((Dt,)), 'ln_b': jnp.zeros((Dt,)), 'fc_W': s(ks[11], Dt, Dt), 'fc_b': jnp.zeros((Dt,))}
        return inp
    _L1_xattn_all = _L1_xattn_setup()
    _L1_xattn_in = {k: v for k, v in _L1_xattn_all.items() if k in ('a_ln1_g', 'a_ln1_b', 'a_ln2_g', 'a_ln2_b', 'a_Wq', 'a_bq', 'a_Wk', 'a_bk', 'a_Wv', 'a_bv', 'a_Wo', 'a_bo', 'v_ln1_g', 'v_ln1_b', 'v_ln2_g', 'v_ln2_b', 'v_Wq', 'v_bq', 'v_Wk', 'v_bk', 'v_Wv', 'v_bv', 'v_Wo', 'v_bo', 'ln_g', 'ln_b', 'fc_W', 'fc_b')}
    del _L1_xattn_all

    def _L2_xattn_setup():
        import jax, jax.numpy as jnp
        import numpy as np
        B, T, E = (8, 1024, 256)
        M, L = (64, 128)
        EPS = 1e-06
        key = jax.random.key(seed)
        ks = jax.random.split(key, 5)
        return {'emb': jax.random.normal(ks[0], (B, T, E), dtype=jnp.float32), 'latent': jax.random.normal(ks[1], (B, M, L), dtype=jnp.float32), 'Wq': jax.random.normal(ks[2], (E, E), dtype=jnp.float32) * (1.0 / np.sqrt(E)), 'bq': jnp.zeros((E,), dtype=jnp.float32), 'Wk': jax.random.normal(ks[3], (L, E), dtype=jnp.float32) * (1.0 / np.sqrt(L)), 'bk': jnp.zeros((E,), dtype=jnp.float32), 'Wv': jax.random.normal(ks[4], (L, E), dtype=jnp.float32) * (1.0 / np.sqrt(L)), 'bv': jnp.zeros((E,), dtype=jnp.float32), 'gamma': jnp.ones((E,), dtype=jnp.float32), 'beta': jnp.zeros((E,), dtype=jnp.float32)}
    _L2_xattn_all = _L2_xattn_setup()
    _L2_xattn_in = {k: v for k, v in _L2_xattn_all.items() if k in ('Wq', 'bq', 'Wk', 'bk', 'Wv', 'bv', 'gamma', 'beta')}
    del _L2_xattn_all

    def _L3_xattn_setup():
        import jax, jax.numpy as jnp
        import numpy as np
        QUERY_DIM = 256
        KEY_DIM = 128
        HIDDEN_DIM = 256
        B, LQ, LK = (8, 512, 512)
        key = jax.random.key(seed)
        ks = jax.random.split(key, 10)
        s_q = 1.0 / np.sqrt(QUERY_DIM)
        s_k = 1.0 / np.sqrt(KEY_DIM)
        s_h = 1.0 / np.sqrt(HIDDEN_DIM)
        return {'query': jax.random.normal(ks[0], (B, LQ, QUERY_DIM), jnp.float32), 'key': jax.random.normal(ks[1], (B, LK, KEY_DIM), jnp.float32), 'Wq': jax.random.uniform(ks[2], (QUERY_DIM, HIDDEN_DIM), jnp.float32, -s_q, s_q), 'bq': jax.random.uniform(ks[3], (HIDDEN_DIM,), jnp.float32, -s_q, s_q), 'Wk': jax.random.uniform(ks[4], (KEY_DIM, HIDDEN_DIM), jnp.float32, -s_k, s_k), 'bk': jax.random.uniform(ks[5], (HIDDEN_DIM,), jnp.float32, -s_k, s_k), 'Wv': jax.random.uniform(ks[6], (KEY_DIM, HIDDEN_DIM), jnp.float32, -s_k, s_k), 'bv': jax.random.uniform(ks[7], (HIDDEN_DIM,), jnp.float32, -s_k, s_k), 'Wo': jax.random.uniform(ks[8], (HIDDEN_DIM, QUERY_DIM), jnp.float32, -s_h, s_h), 'bo': jax.random.uniform(ks[9], (QUERY_DIM,), jnp.float32, -s_h, s_h)}
    _L3_xattn_all = _L3_xattn_setup()
    _L3_xattn_in = {k: v for k, v in _L3_xattn_all.items() if k in ('Wq', 'bq', 'Wk', 'bk', 'Wv', 'bv', 'Wo', 'bo')}
    del _L3_xattn_all
    return {'x': x, 'ctx_512': ctx_512, 'fside_BxSxS_0': fside_BxSxS_0, 'L0_xattn_Wq': _L0_xattn_in['Wq'], 'L0_xattn_bq': _L0_xattn_in['bq'], 'L0_xattn_Wk': _L0_xattn_in['Wk'], 'L0_xattn_bk': _L0_xattn_in['bk'], 'L0_xattn_Wv': _L0_xattn_in['Wv'], 'L0_xattn_bv': _L0_xattn_in['bv'], 'L0_xattn_Wo': _L0_xattn_in['Wo'], 'L0_xattn_bo': _L0_xattn_in['bo'], 'L1_xattn_a_ln1_g': _L1_xattn_in['a_ln1_g'], 'L1_xattn_a_ln1_b': _L1_xattn_in['a_ln1_b'], 'L1_xattn_a_ln2_g': _L1_xattn_in['a_ln2_g'], 'L1_xattn_a_ln2_b': _L1_xattn_in['a_ln2_b'], 'L1_xattn_a_Wq': _L1_xattn_in['a_Wq'], 'L1_xattn_a_bq': _L1_xattn_in['a_bq'], 'L1_xattn_a_Wk': _L1_xattn_in['a_Wk'], 'L1_xattn_a_bk': _L1_xattn_in['a_bk'], 'L1_xattn_a_Wv': _L1_xattn_in['a_Wv'], 'L1_xattn_a_bv': _L1_xattn_in['a_bv'], 'L1_xattn_a_Wo': _L1_xattn_in['a_Wo'], 'L1_xattn_a_bo': _L1_xattn_in['a_bo'], 'L1_xattn_v_ln1_g': _L1_xattn_in['v_ln1_g'], 'L1_xattn_v_ln1_b': _L1_xattn_in['v_ln1_b'], 'L1_xattn_v_ln2_g': _L1_xattn_in['v_ln2_g'], 'L1_xattn_v_ln2_b': _L1_xattn_in['v_ln2_b'], 'L1_xattn_v_Wq': _L1_xattn_in['v_Wq'], 'L1_xattn_v_bq': _L1_xattn_in['v_bq'], 'L1_xattn_v_Wk': _L1_xattn_in['v_Wk'], 'L1_xattn_v_bk': _L1_xattn_in['v_bk'], 'L1_xattn_v_Wv': _L1_xattn_in['v_Wv'], 'L1_xattn_v_bv': _L1_xattn_in['v_bv'], 'L1_xattn_v_Wo': _L1_xattn_in['v_Wo'], 'L1_xattn_v_bo': _L1_xattn_in['v_bo'], 'L1_xattn_ln_g': _L1_xattn_in['ln_g'], 'L1_xattn_ln_b': _L1_xattn_in['ln_b'], 'L1_xattn_fc_W': _L1_xattn_in['fc_W'], 'L1_xattn_fc_b': _L1_xattn_in['fc_b'], 'L2_xattn_Wq': _L2_xattn_in['Wq'], 'L2_xattn_bq': _L2_xattn_in['bq'], 'L2_xattn_Wk': _L2_xattn_in['Wk'], 'L2_xattn_bk': _L2_xattn_in['bk'], 'L2_xattn_Wv': _L2_xattn_in['Wv'], 'L2_xattn_bv': _L2_xattn_in['bv'], 'L2_xattn_gamma': _L2_xattn_in['gamma'], 'L2_xattn_beta': _L2_xattn_in['beta'], 'L3_xattn_Wq': _L3_xattn_in['Wq'], 'L3_xattn_bq': _L3_xattn_in['bq'], 'L3_xattn_Wk': _L3_xattn_in['Wk'], 'L3_xattn_bk': _L3_xattn_in['bk'], 'L3_xattn_Wv': _L3_xattn_in['Wv'], 'L3_xattn_bv': _L3_xattn_in['bv'], 'L3_xattn_Wo': _L3_xattn_in['Wo'], 'L3_xattn_bo': _L3_xattn_in['bo']}

def reference(x, ctx_512, fside_BxSxS_0, L0_xattn_Wq, L0_xattn_bq, L0_xattn_Wk, L0_xattn_bk, L0_xattn_Wv, L0_xattn_bv, L0_xattn_Wo, L0_xattn_bo, L1_xattn_a_ln1_g, L1_xattn_a_ln1_b, L1_xattn_a_ln2_g, L1_xattn_a_ln2_b, L1_xattn_a_Wq, L1_xattn_a_bq, L1_xattn_a_Wk, L1_xattn_a_bk, L1_xattn_a_Wv, L1_xattn_a_bv, L1_xattn_a_Wo, L1_xattn_a_bo, L1_xattn_v_ln1_g, L1_xattn_v_ln1_b, L1_xattn_v_ln2_g, L1_xattn_v_ln2_b, L1_xattn_v_Wq, L1_xattn_v_bq, L1_xattn_v_Wk, L1_xattn_v_bk, L1_xattn_v_Wv, L1_xattn_v_bv, L1_xattn_v_Wo, L1_xattn_v_bo, L1_xattn_ln_g, L1_xattn_ln_b, L1_xattn_fc_W, L1_xattn_fc_b, L2_xattn_Wq, L2_xattn_bq, L2_xattn_Wk, L2_xattn_bk, L2_xattn_Wv, L2_xattn_bv, L2_xattn_gamma, L2_xattn_beta, L3_xattn_Wq, L3_xattn_bq, L3_xattn_Wk, L3_xattn_bk, L3_xattn_Wv, L3_xattn_bv, L3_xattn_Wo, L3_xattn_bo):
    import jax
    import jax.numpy as jnp

    def _L0_xattn_ref(query, key, Wq, bq, Wk, bk, Wv, bv, Wo, bo):
        import jax, jax.numpy as jnp
        import numpy as np
        QUERY_DIM = 256
        KEY_DIM = 128
        HIDDEN_DIM = 256
        B, LQ, LK = (8, 512, 512)
        scale = HIDDEN_DIM ** (-0.5)
        Q = jnp.einsum('bqd,dh->bqh', query, Wq) + bq
        K = jnp.einsum('bkd,dh->bkh', key, Wk) + bk
        V = jnp.einsum('bkd,dh->bkh', key, Wv) + bv
        scores = jnp.einsum('bqh,bkh->bqk', Q, K) * scale
        weights = jax.nn.softmax(scores, axis=-1)
        attended = jnp.einsum('bqk,bkh->bqh', weights, V)
        out = jnp.einsum('bqh,hd->bqd', attended, Wo) + bo
        return query + out

    def _L1_xattn_ref(text, audio, video, a_ln1_g, a_ln1_b, a_ln2_g, a_ln2_b, a_Wq, a_bq, a_Wk, a_bk, a_Wv, a_bv, a_Wo, a_bo, v_ln1_g, v_ln1_b, v_ln2_g, v_ln2_b, v_Wq, v_bq, v_Wk, v_bk, v_Wv, v_bv, v_Wo, v_bo, ln_g, ln_b, fc_W, fc_b):
        import jax, jax.numpy as jnp
        import numpy as np
        EPS = 1e-05

        def _ln(x, g, b):
            mu = jnp.mean(x, axis=-1, keepdims=True)
            var = jnp.var(x, axis=-1, keepdims=True)
            return (x - mu) * jax.lax.rsqrt(var + EPS) * g + b

        def _cma(x1, x2, ln1_g, ln1_b, ln2_g, ln2_b, Wq, bq, Wk, bk, Wv, bv, Wo, bo):
            e = Wq.shape[1]
            scale = e ** (-0.5)
            x1n = _ln(x1, ln1_g, ln1_b)
            x2n = _ln(x2, ln2_g, ln2_b)
            q = x1n @ Wq + bq
            k = x2n @ Wk + bk
            v = x2n @ Wv + bv
            attn = jax.nn.softmax(jnp.einsum('bqe,bke->bqk', q, k) * scale, axis=-1)
            ctx = jnp.einsum('bqk,bke->bqe', attn, v)
            return ctx @ Wo + bo
        out_a = _cma(text, audio, a_ln1_g, a_ln1_b, a_ln2_g, a_ln2_b, a_Wq, a_bq, a_Wk, a_bk, a_Wv, a_bv, a_Wo, a_bo)
        out_v = _cma(text, video, v_ln1_g, v_ln1_b, v_ln2_g, v_ln2_b, v_Wq, v_bq, v_Wk, v_bk, v_Wv, v_bv, v_Wo, v_bo)
        output = out_a + out_v + text
        residual = output
        output = _ln(output, ln_g, ln_b) @ fc_W + fc_b
        return output + residual

    def _L2_xattn_ref(emb, latent, Wq, bq, Wk, bk, Wv, bv, gamma, beta):
        import jax, jax.numpy as jnp
        import numpy as np
        B, T, E = (8, 1024, 256)
        M, L = (64, 128)
        EPS = 1e-06
        q = jnp.einsum('bte,ef->btf', emb, Wq) + bq
        k = jnp.einsum('bml,le->bme', latent, Wk) + bk
        v = jnp.einsum('bml,le->bme', latent, Wv) + bv
        scale = 1.0 / jnp.sqrt(jnp.asarray(E, dtype=q.dtype))
        w = jnp.einsum('bte,bme->btm', q, k) * scale
        w = jax.nn.softmax(w, axis=1)
        pred = jnp.einsum('btm,bme->bte', w, v)
        x = pred + emb
        mu = jnp.mean(x, axis=-1, keepdims=True)
        var = jnp.var(x, axis=-1, keepdims=True)
        return (x - mu) * jax.lax.rsqrt(var + EPS) * gamma + beta

    def _L3_xattn_ref(query, key, Wq, bq, Wk, bk, Wv, bv, Wo, bo):
        import jax, jax.numpy as jnp
        import numpy as np
        QUERY_DIM = 256
        KEY_DIM = 128
        HIDDEN_DIM = 256
        B, LQ, LK = (8, 512, 512)
        scale = HIDDEN_DIM ** (-0.5)
        Q = jnp.einsum('bqd,dh->bqh', query, Wq) + bq
        K = jnp.einsum('bkd,dh->bkh', key, Wk) + bk
        V = jnp.einsum('bkd,dh->bkh', key, Wv) + bv
        scores = jnp.einsum('bqh,bkh->bqk', Q, K) * scale
        weights = jax.nn.softmax(scores, axis=-1)
        attended = jnp.einsum('bqk,bkh->bqh', weights, V)
        out = jnp.einsum('bqh,hd->bqd', attended, Wo) + bo
        return query + out
    x = _L0_xattn_ref(x, ctx_512, L0_xattn_Wq, L0_xattn_bq, L0_xattn_Wk, L0_xattn_bk, L0_xattn_Wv, L0_xattn_bv, L0_xattn_Wo, L0_xattn_bo)
    x = _L1_xattn_ref(x, ctx_512, fside_BxSxS_0, L1_xattn_a_ln1_g, L1_xattn_a_ln1_b, L1_xattn_a_ln2_g, L1_xattn_a_ln2_b, L1_xattn_a_Wq, L1_xattn_a_bq, L1_xattn_a_Wk, L1_xattn_a_bk, L1_xattn_a_Wv, L1_xattn_a_bv, L1_xattn_a_Wo, L1_xattn_a_bo, L1_xattn_v_ln1_g, L1_xattn_v_ln1_b, L1_xattn_v_ln2_g, L1_xattn_v_ln2_b, L1_xattn_v_Wq, L1_xattn_v_bq, L1_xattn_v_Wk, L1_xattn_v_bk, L1_xattn_v_Wv, L1_xattn_v_bv, L1_xattn_v_Wo, L1_xattn_v_bo, L1_xattn_ln_g, L1_xattn_ln_b, L1_xattn_fc_W, L1_xattn_fc_b)
    x = _L2_xattn_ref(x, ctx_512, L2_xattn_Wq, L2_xattn_bq, L2_xattn_Wk, L2_xattn_bk, L2_xattn_Wv, L2_xattn_bv, L2_xattn_gamma, L2_xattn_beta)
    x = _L3_xattn_ref(x, ctx_512, L3_xattn_Wq, L3_xattn_bq, L3_xattn_Wk, L3_xattn_bk, L3_xattn_Wv, L3_xattn_bv, L3_xattn_Wo, L3_xattn_bo)
    return x

_drawn_inputs = setup_inputs


def setup_inputs(seed=0):
    import zlib

    import numpy as np

    out = dict(_drawn_inputs(seed))
    spreads = {'L1_xattn_a_ln1_g': (1.0, 0.6),
     'L1_xattn_a_ln1_b': (0.0, 0.8),
     'L1_xattn_a_ln2_g': (1.0, 0.6),
     'L1_xattn_a_ln2_b': (0.0, 0.8),
     'L1_xattn_a_bq': (0.0, 2.0),
     'L1_xattn_a_bk': (0.0, 2.0),
     'L1_xattn_a_bv': (0.0, 0.291),
     'L1_xattn_a_bo': (0.0, 0.1),
     'L1_xattn_v_ln1_g': (1.0, 0.6),
     'L1_xattn_v_ln1_b': (0.0, 0.8),
     'L1_xattn_v_ln2_g': (1.0, 0.6),
     'L1_xattn_v_ln2_b': (0.0, 0.8),
     'L1_xattn_v_bq': (0.0, 0.8),
     'L1_xattn_v_bk': (0.0, 2.0),
     'L1_xattn_v_bv': (0.0, 0.321),
     'L1_xattn_v_bo': (0.0, 0.1),
     'L1_xattn_ln_g': (1.0, 0.2),
     'L1_xattn_ln_b': (0.0, 0.288),
     'L1_xattn_fc_b': (0.0, 0.1),
     'L2_xattn_bq': (0.0, 2.0),
     'L2_xattn_bk': (0.0, 0.1),
     'L2_xattn_bv': (0.0, 0.1),
     'L2_xattn_gamma': (1.0, 0.2),
     'L2_xattn_beta': (0.0, 0.1)}
    factors = {'fside_BxSxS_0': 8.0,
     'L0_xattn_Wq': 2.973,
     'L0_xattn_bq': 8.0,
     'L0_xattn_Wk': 2.974,
     'L0_xattn_bk': 64.0,
     'L1_xattn_a_Wq': 8.0,
     'L1_xattn_a_Wk': 8.0,
     'L1_xattn_v_Wq': 8.0,
     'L1_xattn_v_Wk': 8.0,
     'L1_xattn_v_Wv': 6.917,
     'L3_xattn_Wq': 2.681,
     'L3_xattn_bq': 40.717,
     'L3_xattn_bk': 64.0}
    for name, (base, spread) in spreads.items():
        noise = np.random.default_rng([zlib.crc32(name.encode()), seed]).standard_normal(out[name].shape)
        drawn = base * np.exp(spread * noise) if base else spread * noise
        out[name] = jnp.asarray(drawn.astype(out[name].dtype))
    for name, factor in factors.items():
        out[name] = (out[name] * factor).astype(out[name].dtype)
    return out
```

```python
from contextlib import ExitStack

import concourse.bass as bass
from concourse import mybir

F32 = mybir.dt.float32
F32R = mybir.dt.float32r
ALU = mybir.AluOpType
ACT = mybir.ActivationFunctionType
AX = mybir.AxisListType

P = 128
D = 256
T = D // P
BATCH = 64
GROUP = 4
GROUPS = BATCH // GROUP
TOK = GROUP * P
PER_BANK = 512 // D
BANKS = 8
OUT_BANKS = GROUP // PER_BANK
LEAD = 11
SCALE = float(D) ** -0.5
EPS_L1 = 1e-5
EPS_L2 = 1e-6

ATTENTIONS = ("L0", "L1a", "L1v", "L3")
COLS = ["L0_bq", "L0_bv", "L1a_bq", "L1a_bv", "L1a_g1", "L1a_b1", "L1v_bq", "L1v_bv", "L1v_g1", "L1v_b1",
        "L3_bq", "L3_bv", "L3_g1", "L3_b1", "L2_bk", "fc_g", "fc_b", "L1a_b2", "L1v_b2", "L1a_g2", "L1v_g2"]
ROWS = ["L0_bo", "L1a_bo", "L1v_bo", "L3_bo", "fc_bias", "L2_bv", "L3_b1", "L3_g1", "L1a_g2", "L1v_g2"]


class Marks:

    def __init__(self, nc, stack):
        self.nc, self.stack, self.sems, self.count, self.value = nc, stack, {}, {}, {}

    def raised(self, counter, step, group, increment):
        if counter not in self.sems:
            self.sems[counter] = self.stack.enter_context(self.nc.semaphore("s_" + counter))
            self.count[counter] = 0
        self.count[counter] += increment
        self.value[step, group] = counter, self.count[counter]
        return self.sems[counter]


class Queue:

    def __init__(self, marks, name):
        self.marks, self.name, self.items, self.reached = marks, name, [], {}

    def wait(self, step, group=0):
        if isinstance(group, int) and group < 0:
            return
        counter, value = self.marks.value[step, group]
        if self.reached.get(counter, 0) < value:
            self.reached[counter] = value
            sem = self.marks.sems[counter]
            self.items.append(lambda e: e.wait_ge(sem, value))

    def op(self, method, *args, done=None, **kw):
        if done is None:
            self.items.append(lambda e: method(*args, **kw))
        else:
            sem = self.marks.raised(self.name, *done, 1)
            self.items.append(lambda e: method(*args, **kw).then_inc(sem, 1))

    def dma(self, method, dst, src, done):
        sem = self.marks.raised(done[0], *done, 16)
        self.items.append(lambda e: method(dst, src).then_inc(sem, 16))

    def play(self, e):
        for item in self.items:
            item(e)


class Banks:

    def __init__(self, banks, pe):
        self.banks, self.pe, self.last, self.turn = banks, pe, [[] for _ in banks], 0

    def take(self, *readers):
        n = self.turn % len(self.banks)
        self.turn += 1
        for step, group in self.last[n]:
            self.pe.wait(step, group)
        self.last[n] = readers
        return self.banks[n]


def build(nc, ins, out):
    stack = ExitStack()
    with stack:
        marks = Marks(nc, stack)
        pe, act, dve, pool, sp = (Queue(marks, n) for n in ("pe", "act", "dve", "pool", "sp"))
        mm, tr = nc.tensor.matmul, nc.tensor.transpose

        def sb(name, shape, dtype=F32, where=stack):
            return where.enter_context(nc.sbuf_tensor(name, shape, dtype))

        def ring(name, copies, shape, dtype=F32):
            return [sb(f"{name}_{i}", shape, dtype) for i in range(copies)]

        banks = Banks([stack.enter_context(nc.psum_tensor(f"bank{i}", [P, 512], F32)) for i in range(BANKS)], pe)

        ident = sb("ident", [P, P])
        minus_half = sb("minus_half", [P, GROUP])
        ones_r = sb("ones_r", [P, P], F32R)
        cols = sb("cols", [P, len(COLS), T])
        gamma_row = sb("gamma_row", [P, D])
        M_hi = {a: sb(f"M_hi_{a}", [P, T, P], F32R) for a in ATTENTIONS}
        M_lo = {a: sb(f"M_lo_{a}", [P, T, P], F32R) for a in ATTENTIONS}
        N_hi = {a: sb(f"N_hi_{a}", [P, D], F32R) for a in ATTENTIONS}
        N_lo = {a: sb(f"N_lo_{a}", [P, D], F32R) for a in ATTENTIONS}
        m_col = {a: sb(f"m_{a}", [P, 1]) for a in ATTENTIONS}
        F_hi, F_lo = sb("F_hi", [P, T, D], F32R), sb("F_lo", [P, T, D], F32R)
        M2T, Wv2, k_bias2 = sb("M2T", [P, D]), sb("Wv2", [P, D]), sb("k_bias2", [P, T])
        bias_hl = {k: sb(f"bias_{k}", [P, D], F32R) for k in ("L0", "L1", "fc", "L2v", "L3")}

        x_in = ring("x_in", 2, [P, GROUP, D])
        ctx_in = ring("ctx_in", 4, [P, GROUP, P])
        side_in = ring("side_in", 2, [P, GROUP, P])
        ctxT = ring("ctxT", 4, [P, TOK])
        keys = {"L1a": ring("chat", 2, [P, GROUP, P]), "L1v": ring("vhat", 2, [P, GROUP, P])}
        keysT = {"L1a": ring("chatT", 2, [P, TOK]), "L1v": ring("vhatT", 2, [P, TOK])}
        V2 = ring("V2", 2, [P, GROUP, D])
        B2 = ring("B2", 2, [P, T, TOK])
        xT_hi = {k: ring(f"xT_hi_{k}", 1, [P, T, TOK], F32R) for k in ("L0", "L1", "fc")}
        xT_lo = {k: ring(f"xT_lo_{k}", 1, [P, T, TOK], F32R) for k in ("L0", "L1", "fc")}
        qT = {k: ring(f"qT_{k}", 1, [P, TOK]) for k in ("L0", "L1a", "L1v")}
        prob = {k: ring(f"prob_{k}", 1, [P, GROUP, P]) for k in ("L0", "L1a", "L1v")}
        probT = {k: ring(f"probT_{k}", 1, [P, TOK]) for k in ("L0", "L1a", "L1v")}
        oT_hi = {k: ring(f"oT_hi_{k}", 1, [P, TOK], F32R) for k in ("L0", "L1a", "L1v")}
        oT_lo = {k: ring(f"oT_lo_{k}", 1, [P, TOK], F32R) for k in ("L0", "L1a", "L1v")}
        x1 = ring("x1", 1, [P, GROUP, D])
        x2 = ring("x2", 1, [P, GROUP, D])
        stats = {k: ring(f"stats_{k}", 2, [P, GROUP, 6]) for k in ("ctx", "side", "ln1", "lnf", "ln2")}
        mean_var = {k: ring(f"mv_{k}", 2, [P, GROUP, 2]) for k in stats}
        var_eps = {k: ring(f"ve_{k}", 2, [P, GROUP]) for k in stats}
        rstd = {k: ring(f"rstd_{k}", 2, [P, GROUP]) for k in stats}
        shift = {k: ring(f"shift_{k}", 2, [P, GROUP]) for k in stats}
        softmaxes = ("L0", "L1a", "L1v", "L2", "L3")
        neg_max = {k: ring(f"neg_max_{k}", 2, [P, GROUP]) for k in softmaxes}
        total = {k: ring(f"total_{k}", 2, [P, GROUP]) for k in softmaxes}
        inv_total = {k: ring(f"inv_{k}", 2, [P, GROUP]) for k in softmaxes}

        with ExitStack() as staging:
            stage = {}
            for a in ATTENTIONS:
                stage[a] = {"WqT": sb(f"WqT_{a}", [P, T, D], where=staging), "WkT": sb(f"WkT_{a}", [P, T, P], where=staging),
                            "WvT": sb(f"WvT_{a}", [P, T, P], where=staging), "Wo": sb(f"Wo_{a}", [P, T, D], where=staging)}
            stage["L2"] = {"WqT": sb("WqT_L2", [P, T, D], where=staging), "WkT": sb("WkT_L2", [P, T, P], where=staging)}
            fcW = sb("fcW", [P, T, D], where=staging)
            rows = sb("rows", [P, len(ROWS), D], where=staging)
            rep = sb("rep", [P, T, P], where=staging)
            rep2 = sb("rep2", [P, P], where=staging)
            M0 = sb("M0", [P, T, P], where=staging)
            Mg = sb("Mg", [P, T, P], where=staging)
            N0 = sb("N0", [P, D], where=staging)
            Ng = sb("Ng", [P, D], where=staging)
            Fg = sb("Fg", [P, T, D], where=staging)
            bias_full = sb("bias_full", [P, D], where=staging)
            bias_hi = sb("bias_hi", [P, D], F32R, where=staging)
        x3 = ring("x3", 1, [P, GROUP, D])
        xhat = {"ln1": ring("xhat_ln1", 1, [P, GROUP, D]), "lnf": ring("xhat_lnf", 1, [P, GROUP, D]),
                "ln2": ring("xhat_ln2", 1, [P, GROUP, D])}
        xT2 = ring("xT2", 1, [P, T, TOK])
        x4 = ring("x4", 1, [P, GROUP, D])
        x_res = ring("x_res", 1, [P, GROUP, D])
        xT_hi["L3"] = ring("xT_hi_L3", 1, [P, T, TOK], F32R)
        xT_lo["L3"] = ring("xT_lo_L3", 1, [P, T, TOK], F32R)
        for name, buffers in (("qT", qT), ("probT", probT)):
            buffers["L3"] = ring(f"{name}_L3", 1, [P, TOK])
        for k in ("L2", "L3"):
            prob[k] = ring(f"prob_{k}", 1, [P, GROUP, P])
        oT_hi["L3"] = ring("oT_hi_L3", 1, [P, TOK], F32R)
        oT_lo["L3"] = ring("oT_lo_L3", 1, [P, TOK], F32R)
        y = ring("y", 1, [P, GROUP, D])

        def at(buffers, g):
            return buffers[g % len(buffers)]

        def f32(tile):
            return tile[:].bitcast(F32)

        def col(name, t=0):
            n = COLS.index(name)
            return cols[:, n, t:t + 1]

        def row(name, width=D):
            return rows[:, ROWS.index(name), 0:width]

        def load(dst, src, step):
            sp.dma(nc.sync.dma_start, dst, src, done=(step, 0))

        def load_weights(a):
            for w in stage[a]:
                load(stage[a][w][:], ins[f"{a}_{w}"].rearrange("(t p) n -> p t n", p=P), f"w_{a}")

        def constants():
            pool.op(nc.gpsimd.memset, ident[:], 0.0, done=("zeroed", 0))
            pool.wait("zeroed")
            pool.op(nc.gpsimd.affine_select, out=ident[:], in_=ident[:], compare_op=ALU.not_equal, fill=1.0,
                    base=0, pattern=[[-1, P]], channel_multiplier=1, done=("ident", 0))
            pool.op(nc.gpsimd.memset, minus_half[:], -0.5)
            pool.op(nc.gpsimd.memset, ones_r[:].bitcast(F32), 1.0)
            for k in bias_hl:
                pool.op(nc.gpsimd.memset, bias_hl[k][:].bitcast(F32), 0.0, done=("constants", 0))

        chain = [0]

        def link(method, *args, **kw):
            chain[0] += 1
            dve.op(method, *args, done=("prep_v", chain[0]), **kw)
            dve.wait("prep_v", chain[0])

        def pe_to_dve(step):
            pe.wait("prep_v", chain[0])

        v = nc.vector

        def split(hi, lo, full):
            link(v.tensor_copy, hi[:], full[:])
            link(v.tensor_tensor, lo[:], full[:], f32(hi), ALU.subtract)

        def bias_row(key, psum, extra):
            first = extra[0]
            if psum is not None:
                link(v.tensor_tensor, bias_full[:], psum[:, 0:D], row(first), ALU.add)
            else:
                link(v.tensor_copy, bias_full[:], row(first))
            for r in extra[1:]:
                link(v.tensor_tensor, bias_full[:], bias_full[:], row(r), ALU.add)
            dve.wait("constants")
            link(v.tensor_copy, bias_hi[:], bias_full[:])
            link(v.tensor_copy, bias_hl[key][0:1, :], bias_full[0:1, :])
            link(v.tensor_tensor, bias_hl[key][32:33, :], bias_full[32:33, :], bias_hi[32:33, :].bitcast(F32), ALU.subtract)

        def prep_attention(a, n_bank, first, last):
            w = stage[a]
            ln = a != "L0"
            ln_keys = a in ("L1a", "L1v")
            dve.wait("vectors")
            dve.wait(f"w_{a}")
            for t in range(T):
                if ln_keys:
                    link(v.scalar_tensor_tensor, out=w["WkT"][:, t, :], in0=w["WkT"][:, t, :], scalar=SCALE,
                         in1=row(f"{a}_g2", P), op0=ALU.mult, op1=ALU.mult)
                else:
                    link(v.tensor_scalar, w["WkT"][:, t, :], w["WkT"][:, t, :], SCALE, None, ALU.mult)
            for t in range(T):
                link(v.tensor_copy, rep[:, t, :], col(f"{a}_bv", t).to_broadcast([P, P]))
            if ln_keys:
                link(v.tensor_copy, rep2[:], col(f"{a}_b2").to_broadcast([P, P]))
            pe.wait("prep_v", chain[0])
            pe.wait(f"w_{a}")
            bank = banks.take(("prep_M", a))
            for e in range(T):
                for h in range(T):
                    pe.op(mm, bank[:, e * P:(e + 1) * P], w["WqT"][:, h, e * P:(e + 1) * P], w["WkT"][:, h, :],
                          start=h == 0, stop=h == T - 1, done=("prep_pe", f"M{a}{e}{h}"))
            dve.wait("prep_pe", f"M{a}{T - 1}{T - 1}")
            dve.op(v.tensor_copy, M0[:], bank[:, 0:T * P].rearrange("p (t d) -> p t d", t=T), done=("prep_M", a))
            dve.wait("prep_M", a)
            if ln:
                for t in range(T):
                    link(v.tensor_scalar, Mg[:, t, :], M0[:, t, :], col(f"{a}_g1", t), None, ALU.mult)
            split(M_hi[a], M_lo[a], Mg if ln else M0)
            pe.wait("prep_M", a)
            bank = banks.take(("prep_m", a))
            for h in range(T):
                pe.op(mm, bank[:, 0:1], w["WkT"][:, h, :], col(f"{a}_bq", h), start=h == 0, stop=h == T - 1 and not ln,
                      done=("prep_pe", f"m{a}{h}"))
            if ln:
                for e in range(T):
                    pe.op(mm, bank[:, 0:1], M0[:, e, :], col(f"{a}_b1", e), start=False, stop=e == T - 1,
                          done=("prep_pe", f"m{a}{T - 1}"))
            dve.wait("prep_pe", f"m{a}{T - 1}")
            dve.op(v.tensor_copy, m_col[a][:], bank[:, 0:1], done=("prep_m", a))
            bank = banks.take(("prep_N", a))
            for h in range(T):
                pe.op(mm, bank[:, 0:D], w["WvT"][:, h, :], w["Wo"][:, h, :], start=h == 0, stop=h == T - 1,
                      done=("prep_pe", f"N{a}{h}"))
            dve.wait("prep_pe", f"N{a}{T - 1}")
            dve.op(v.tensor_copy, N0[:], bank[:, 0:D], done=("prep_N", a))
            dve.wait("prep_N", a)
            if ln_keys:
                link(v.tensor_scalar, Ng[:], N0[:], col(f"{a}_g2"), None, ALU.mult)
            split(N_hi[a], N_lo[a], Ng if ln_keys else N0)
            for h in range(T):
                pe.op(mm, n_bank[:, 0:D], rep[:, h, :], w["Wo"][:, h, :], start=first and h == 0,
                      stop=last and not ln_keys and h == T - 1, done=("prep_pe", f"n{a}{h}"))
            if ln_keys:
                pe.wait("prep_N", a)
                pe.op(mm, n_bank[:, 0:D], rep2[:], N0[:], start=False, stop=last, done=("prep_pe", f"n{a}{T - 1}"))
            dve.wait("prep_pe", f"n{a}{T - 1}")

        def prep_L0():
            bank = banks.take(("prep_v", "bias_L0"))
            prep_attention("L0", bank, True, True)
            bias_row("L0", bank, ["L0_bo"])
            marks.value["prep_v", "bias_L0"] = marks.value["prep_v", chain[0]]

        def prep_L3():
            bank = banks.take(("prep_v", "bias_L3"))
            prep_attention("L3", bank, True, True)
            bias_row("L3", bank, ["L3_bo", "L3_b1"])
            marks.value["prep_v", "bias_L3"] = marks.value["prep_v", chain[0]]
            link(v.tensor_copy, gamma_row[:], row("L3_g1"))

        def prep_L1():
            bank = banks.take(("prep_v", "bias_L1"))
            prep_attention("L1a", bank, True, False)
            prep_attention("L1v", bank, False, True)
            bias_row("L1", bank, ["L1a_bo", "L1v_bo"])
            marks.value["prep_v", "bias_L1"] = marks.value["prep_v", chain[0]]

        def prep_fc():
            dve.wait("w_fc")
            for t in range(T):
                link(v.tensor_scalar, Fg[:, t, :], fcW[:, t, :], col("fc_g", t), None, ALU.mult)
            split(F_hi, F_lo, Fg)
            for t in range(T):
                link(v.tensor_copy, rep[:, t, :], col("fc_b", t).to_broadcast([P, P]))
            pe.wait("prep_v", chain[0])
            bank = banks.take(("prep_v", "bias_fc"))
            for t in range(T):
                pe.op(mm, bank[:, 0:D], rep[:, t, :], fcW[:, t, :], start=t == 0, stop=t == T - 1, done=("prep_pe", f"f{t}"))
            dve.wait("prep_pe", f"f{T - 1}")
            bias_row("fc", bank, ["fc_bias"])
            marks.value["prep_v", "bias_fc"] = marks.value["prep_v", chain[0]]

        def prep_L2():
            w = stage["L2"]
            dve.wait("vectors")
            dve.wait("w_L2")
            for t in range(T):
                link(v.tensor_scalar, w["WkT"][:, t, :], w["WkT"][:, t, :], SCALE, None, ALU.mult)
            pe.wait("prep_v", chain[0])
            pe.wait("w_L2")
            bank = banks.take(("prep_M", "L2"))
            for h in range(T):
                pe.op(mm, bank[:, 0:D], w["WkT"][:, h, :], w["WqT"][:, h, :], start=h == 0, stop=h == T - 1,
                      done=("prep_pe", f"M2{h}"))
            dve.wait("prep_pe", f"M2{T - 1}")
            dve.op(v.tensor_copy, M2T[:], bank[:, 0:D], done=("prep_M", "L2"))
            bank = banks.take(("prep_v", "bias_L2k"))
            for e in range(T):
                for h in range(T):
                    pe.op(mm, bank[:, e:e + 1], w["WqT"][:, h, e * P:(e + 1) * P], col("L2_bk", h),
                          start=h == 0, stop=h == T - 1, done=("prep_pe", f"k2{e}{h}"))
            dve.wait("prep_pe", f"k2{T - 1}{T - 1}")
            link(v.tensor_scalar, k_bias2[:], bank[:, 0:T], SCALE, None, ALU.mult)
            marks.value["prep_v", "bias_L2k"] = marks.value["prep_v", chain[0]]
            bias_row("L2v", None, ["L2_bv"])

        def evacuate(engine, step, g, dst, bank, bias=None):
            if engine is act:
                if bias is None:
                    act.op(nc.scalar.activation, dst, bank, ACT.Copy, done=(step, g))
                else:
                    act.op(nc.scalar.activation, dst, bank, ACT.Identity, bias=bias, done=(step, g))
            elif bias is None:
                dve.op(v.tensor_copy, dst, bank, done=(step, g))
            else:
                dve.op(v.tensor_scalar, dst, bank, bias, None, ALU.add, done=(step, g))

        def transposed(k, g, src, ready, hi, lo, free, engine=act):
            pe.wait(*ready)
            for t in range(T):
                bank = banks.take((f"lo_{k}{t}" if lo else f"hi_{k}{t}", g))
                for b in range(GROUP):
                    pe.op(tr, bank[:, b * P:(b + 1) * P], src[:, b, t * P:(t + 1) * P], ident[:],
                          done=(f"T_{k}{t}", g) if b == GROUP - 1 else None)
                engine.wait(f"T_{k}{t}", g)
                engine.wait(*free)
                evacuate(engine, f"hi_{k}{t}", g, hi[:, t, :], bank[:])
                if lo:
                    dve.wait(f"hi_{k}{t}", g)
                    dve.wait(*free)
                    dve.op(v.tensor_tensor, lo[:, t, :], bank[:], hi[:, t, :].bitcast(F32), ALU.subtract,
                           done=(f"lo_{k}{t}", g))

        def queries(a, k, g, hi, lo):
            bank = banks.take((f"q_{a}", g))
            n = 0
            for t in range(T):
                pe.wait(f"hi_{k}{t}", g)
                pe.wait(f"lo_{k}{t}", g)
                for w, x in ((M_hi[a], hi), (M_lo[a], hi), (M_hi[a], lo)):
                    n += 1
                    pe.op(mm, bank[:], w[:, t, :], x[:, t, :], start=n == 1, stop=n == 3 * T,
                          done=(f"Q_{a}", g) if n == 3 * T else None)
            act.wait(f"Q_{a}", g)
            act.wait(f"S_{a}", g - 1)
            evacuate(act, f"q_{a}", g, at(qT[a], g)[:], bank[:], bias=m_col[a][:, 0:1])

        def scores(a, g, kT):
            pe.wait(f"q_{a}", g)
            bank = banks.take((f"exp_{a}", g))
            for b in range(GROUP):
                s = slice(b * P, (b + 1) * P)
                pe.op(mm, bank[:, s], at(qT[a], g)[:, s], kT[:, s], start=True, stop=True,
                      done=(f"S_{a}", g) if b == GROUP - 1 else None)
            return bank

        def softmax(a, g, bank, read_by):
            dve.wait(f"S_{a}", g)
            dve.wait(f"exp_{a}", g - 2)
            dve.op(v.tensor_reduce, at(neg_max[a], g)[:], bank[:].rearrange("p (b k) -> p b k", k=P), AX.X, ALU.max,
                   negate=True, done=(f"max_{a}", g))
            act.wait(f"max_{a}", g)
            act.wait(read_by, g - 1)
            act.wait(f"inv_{a}", g - 2)
            dst = at(prob[a], g)
            for b in range(GROUP):
                act.op(nc.scalar.activation, dst[:, b, :], bank[:, b * P:(b + 1) * P], ACT.Exp,
                       bias=at(neg_max[a], g)[:, b:b + 1], accum_out=at(total[a], g)[:, b:b + 1],
                       done=(f"exp_{a}", g) if b == GROUP - 1 else None)
            dve.wait(f"exp_{a}", g)
            dve.wait(f"prob_{a}", g - 2)
            dve.op(v.reciprocal, at(inv_total[a], g)[:], at(total[a], g)[:], done=(f"inv_{a}", g))
            pool.wait(f"inv_{a}", g)
            for b in range(GROUP):
                pool.op(nc.gpsimd.tensor_scalar, dst[:, b, :], dst[:, b, :], at(inv_total[a], g)[:, b:b + 1], 1.0,
                        ALU.mult, ALU.mult, done=(f"prob_{a}", g) if b == GROUP - 1 else None)

        def prob_transposed(a, g, engine):
            pe.wait(f"prob_{a}", g)
            bank = banks.take((f"pT_{a}", g))
            for b in range(GROUP):
                pe.op(tr, bank[:, b * P:(b + 1) * P], at(prob[a], g)[:, b, :], ident[:],
                      done=(f"PT_{a}", g) if b == GROUP - 1 else None)
            engine.wait(f"PT_{a}", g)
            engine.wait(f"O_{a}", g - 1)
            evacuate(engine, f"pT_{a}", g, at(probT[a], g)[:], bank[:])

        def attended(a, g, natural):
            out_step = "OUT_L1" if a in ("L1a", "L1v") else f"OUT_{a}"
            pe.wait(f"pT_{a}", g)
            bank = banks.take((f"o_lo_{a}", g))
            for b in range(GROUP):
                s = slice(b * P, (b + 1) * P)
                pe.op(mm, bank[:, s], natural[:, b, :], at(probT[a], g)[:, s], start=True, stop=True,
                      done=(f"O_{a}", g) if b == GROUP - 1 else None)
            act.wait(f"O_{a}", g)
            act.wait(out_step, g - 1)
            evacuate(act, f"o_hi_{a}", g, at(oT_hi[a], g)[:], bank[:])
            dve.wait(f"o_hi_{a}", g)
            dve.wait(out_step, g - 1)
            dve.op(v.tensor_tensor, at(oT_lo[a], g)[:], bank[:], f32(at(oT_hi[a], g)), ALU.subtract,
                   done=(f"o_lo_{a}", g))

        def wide_bias(key, bank):
            pe.op(mm, bank[:], ones_r[:], bias_hl[key][:].unsqueeze(1).to_broadcast([P, PER_BANK, D]),
                  start=True, stop=False)

        def project(k, key, g, attentions, add, dst, free):
            for n in range(OUT_BANKS):
                bank = banks.take((f"out_{k}{n}", g))
                wide_bias(key, bank)
                for a in attentions:
                    pe.wait(f"o_lo_{a}", g)
                    hi, lo = at(oT_hi[a], g), at(oT_lo[a], g)
                    for j in range(PER_BANK):
                        s = slice((n * PER_BANK + j) * P, (n * PER_BANK + j + 1) * P)
                        for o, w in ((hi, N_hi[a]), (hi, N_lo[a]), (lo, N_hi[a])):
                            last = a == attentions[-1] and j == PER_BANK - 1 and w is N_hi[a] and o is lo
                            pe.op(mm, bank[:, j * D:(j + 1) * D], o[:, s], w[:], start=False, stop=last,
                                  done=(f"OUT_{k}", g if n == OUT_BANKS - 1 else (g, n)) if last else None)
                residual(k, n, g, bank, add, dst, free)

        def residual(k, n, g, bank, add, dst, free):
            dve.wait(f"OUT_{k}", g if n == OUT_BANKS - 1 else (g, n))
            for step, group in free:
                dve.wait(step, group)
            b = slice(n * PER_BANK, (n + 1) * PER_BANK)
            dve.op(v.tensor_tensor, dst[:, b, :], bank[:].rearrange("p (b d) -> p b d", d=D), add[:, b, :], ALU.add,
                   done=(f"out_{k}{n}", g))

        def norm_stats(k, g, src, eps, written_by=()):
            st, mv = at(stats[k], g), at(mean_var[k], g)
            for step in written_by:
                dve.wait(step, g)
            for b in range(GROUP):
                dve.op(v.bn_stats, st[:, b, :], src[:, b, :], done=(f"st_{k}", g) if b == GROUP - 1 else None)
            dve.wait(f"st_{k}", g)
            for b in range(GROUP):
                dve.op(v.bn_aggr, mv[:, b, :], st[:, b, :], done=(f"mv_{k}", g) if b == GROUP - 1 else None)
            dve.wait(f"mv_{k}", g)
            dve.wait(f"rstd_{k}", g - 2)
            dve.op(v.tensor_scalar, at(var_eps[k], g)[:], mv[:, :, 1], eps, None, ALU.add, done=(f"ve_{k}", g))
            pool.wait(f"ve_{k}", g)
            pool.wait("constants")
            pool.wait(f"shift_{k}", g - 2)
            pool.op(nc.gpsimd.tensor_tensor, at(rstd[k], g)[:], at(var_eps[k], g)[:], minus_half[:], ALU.pow,
                    done=(f"rstd_{k}", g))

        def written(k):
            return [f"out_{k}{n}" for n in range(OUT_BANKS)]

        def norm_apply(k, g, src, dst, free):
            dve.wait(f"rstd_{k}", g)
            dve.wait(f"norm_{k}", g - 2)
            dve.op(v.scalar_tensor_tensor, out=at(shift[k], g)[:], in0=at(mean_var[k], g)[:, :, 0], scalar=-1.0,
                   in1=at(rstd[k], g)[:], op0=ALU.mult, op1=ALU.mult, done=(f"shift_{k}", g))
            pool.wait(f"shift_{k}", g)
            for step, group in free:
                pool.wait(step, group)
            for b in range(GROUP):
                pool.op(nc.gpsimd.tensor_scalar, dst[:, b, :], src[:, b, :], at(rstd[k], g)[:, b:b + 1],
                        at(shift[k], g)[:, b:b + 1], ALU.mult, ALU.add,
                        done=(f"norm_{k}", g) if b == GROUP - 1 else None)

        def seqs(tensor, g):
            return tensor[g * GROUP:(g + 1) * GROUP].rearrange("b p e -> p b e")

        def load_group(g):
            sp.wait("T_L0" + str(T - 1), g - 2)
            for n in range(OUT_BANKS):
                sp.wait(f"out_L0{n}", g - 2)
            sp.dma(nc.sync.dma_start, at(x_in, g)[:], seqs(ins["x"], g), done=(f"x_in{g % 2}", g))
            sp.wait("O_L3", g - 4)
            sp.dma(nc.sync.dma_start, at(ctx_in, g)[:], seqs(ins["ctx"], g), done=(f"ctx_in{g % 4}", g))
            sp.wait("norm_side", g - 2)
            sp.dma(nc.sync.dma_start, at(side_in, g)[:], seqs(ins["side"], g), done=(f"side_in{g % 2}", g))

        def one_transpose(k, g, src, ready, dst, free, engine):
            pe.wait(*ready)
            bank = banks.take((f"t_{k}", g))
            for b in range(GROUP):
                pe.op(tr, bank[:, b * P:(b + 1) * P], src[:, b, :], ident[:],
                      done=(f"T_{k}", g) if b == GROUP - 1 else None)
            engine.wait(f"T_{k}", g)
            engine.wait(*free)
            evacuate(engine, f"t_{k}", g, dst[:], bank[:])

        def ctx_stats(g):
            dve.wait(f"ctx_in{g % 4}", g)
            norm_stats("ctx", g, at(ctx_in, g), EPS_L1)

        def side_stats(g):
            dve.wait(f"side_in{g % 2}", g)
            norm_stats("side", g, at(side_in, g), EPS_L1)

        def ctx_transposed(g):
            pe.wait("ident")
            one_transpose("ctx", g, at(ctx_in, g), (f"ctx_in{g % 4}", g), at(ctxT, g), ("S_L3", g - 4), act)

        def keys_normed(g):
            pool.wait(f"ctx_in{g % 4}", g)
            norm_apply("ctx", g, at(ctx_in, g), at(keys["L1a"], g), [("O_L1a", g - 2)])
            pool.wait(f"side_in{g % 2}", g)
            norm_apply("side", g, at(side_in, g), at(keys["L1v"], g), [("O_L1v", g - 2)])

        def keys_transposed(g):
            one_transpose("chat", g, at(keys["L1a"], g), ("norm_ctx", g), at(keysT["L1a"], g), ("S_L1a", g - 2), act)
            one_transpose("vhat", g, at(keys["L1v"], g), ("norm_side", g), at(keysT["L1v"], g), ("S_L1v", g - 2), act)

        def values_L2(g):
            pe.wait("t_ctx", g)
            for n in range(OUT_BANKS):
                bank = banks.take((f"v2_{n}", g))
                wide_bias("L2v", bank)
                for j in range(PER_BANK):
                    b = n * PER_BANK + j
                    pe.op(mm, bank[:, j * D:(j + 1) * D], at(ctxT, g)[:, b * P:(b + 1) * P], Wv2[:], start=False,
                          stop=j == PER_BANK - 1, done=(f"V2_{n}", g) if j == PER_BANK - 1 else None)
                act.wait(f"V2_{n}", g)
                act.wait("OUT_L2", g - 2)
                evacuate(act, f"v2_{n}", g, at(V2, g)[:, n * PER_BANK:(n + 1) * PER_BANK, :],
                         bank[:].rearrange("p (b d) -> p b d", d=D))

        def keys_L2(g):
            for e in range(T):
                bank = banks.take((f"b2_{e}", g))
                pe.op(mm, bank[:], M2T[:, e * P:(e + 1) * P], at(ctxT, g)[:], start=True, stop=True,
                      done=(f"B2_{e}", g))
                act.wait(f"B2_{e}", g)
                act.wait("S_L2", g - 2)
                evacuate(act, f"b2_{e}", g, at(B2, g)[:, e, :], bank[:], bias=k_bias2[:, e:e + 1])

        def project_fc(g):
            hi, lo = at(xT_hi["fc"], g), at(xT_lo["fc"], g)
            for t in range(T):
                pe.wait(f"lo_fc{t}", g)
            for n in range(OUT_BANKS):
                bank = banks.take((f"out_fc{n}", g))
                wide_bias("fc", bank)
                for j in range(PER_BANK):
                    s = slice((n * PER_BANK + j) * P, (n * PER_BANK + j + 1) * P)
                    for t in range(T):
                        for i, (o, w) in enumerate(((hi, F_hi), (hi, F_lo), (lo, F_hi))):
                            last = j == PER_BANK - 1 and t == T - 1 and i == 2
                            pe.op(mm, bank[:, j * D:(j + 1) * D], o[:, t, s], w[:, t, :], start=False, stop=last,
                                  done=("OUT_fc", g if n == OUT_BANKS - 1 else (g, n)) if last else None)
                residual("fc", n, g, bank, at(x2, g), at(x3, g), [(f"out_L2{n}", g - 1)])

        def scores_L2(g):
            bank = banks.take(("exp_L2", g))
            for e in range(T):
                pe.wait(f"hi_L2{e}", g)
                pe.wait(f"b2_{e}", g)
            for b in range(GROUP):
                s = slice(b * P, (b + 1) * P)
                for e in range(T):
                    pe.op(mm, bank[:, s], at(B2, g)[:, e, s], at(xT2, g)[:, e, s], start=e == 0, stop=e == T - 1,
                          done=("S_L2", g) if b == GROUP - 1 and e == T - 1 else None)
            return bank

        def attend_L2(g):
            pe.wait("prob_L2", g)
            for n in range(OUT_BANKS):
                pe.wait(f"v2_{n}", g)
                bank = banks.take((f"out_L2{n}", g))
                for j in range(PER_BANK):
                    b = n * PER_BANK + j
                    last = j == PER_BANK - 1
                    pe.op(mm, bank[:, j * D:(j + 1) * D], at(prob["L2"], g)[:, b, :], at(V2, g)[:, b, :],
                          start=True, stop=True,
                          done=("OUT_L2", g if n == OUT_BANKS - 1 else (g, n)) if last else None)
                residual("L2", n, g, bank, at(x3, g), at(x4, g), [("norm_ln2", g - 1)])

        def gamma_residual(g):
            pool.wait("norm_ln2", g)
            for n in range(OUT_BANKS):
                pool.wait(f"out_L3{n}", g - 1)
            pool.op(nc.gpsimd.tensor_tensor, at(x_res, g)[:], at(xhat["ln2"], g)[:],
                    gamma_row[:].unsqueeze(1).to_broadcast([P, GROUP, D]), ALU.mult, done=("x_res", g))

        def store(g):
            for n in range(OUT_BANKS):
                sp.wait(f"out_L3{n}", g)
            sp.dma(nc.sync.dma_start, seqs(out, g), at(y, g)[:], done=(f"stored{g % 2}", g))

        banks_of = {}

        def open_scores(a, g, kT):
            banks_of[a, g] = scores(a, g, kT)

        def transpose_ready(g):
            pe.wait("ident")
            pe.wait(f"x_in{g % 2}", g)

        def l0_residual_ready(g):
            dve.wait(f"x_in{g % 2}", g)

        plan = {
            -12: [load_group],
            -7: [ctx_stats, side_stats],
            -6: [ctx_transposed],
            -5: [keys_normed],
            -4: [keys_transposed],
            0: [transpose_ready,
                lambda g: transposed("L0", g, at(x_in, g), (f"x_in{g % 2}", g), at(xT_hi["L0"], g), at(xT_lo["L0"], g),
                                     ("Q_L0", g - 1))],
            1: [lambda g: queries("L0", "L0", g, at(xT_hi["L0"], g), at(xT_lo["L0"], g))],
            2: [lambda g: pe.wait("t_ctx", g), lambda g: open_scores("L0", g, at(ctxT, g)),
                lambda g: softmax("L0", g, banks_of["L0", g], "PT_L0")],
            4: [lambda g: prob_transposed("L0", g, act)],
            5: [lambda g: attended("L0", g, at(ctx_in, g))],
            6: [l0_residual_ready,
                lambda g: project("L0", "L0", g, ["L0"], at(x_in, g), at(x1, g),
                                  [("norm_ln1", g - 1), ("out_L10", g - 1), (f"out_L1{OUT_BANKS - 1}", g - 1)])],
            7: [lambda g: norm_stats("ln1", g, at(x1, g), EPS_L1, written("L0")), values_L2],
            8: [lambda g: norm_apply("ln1", g, at(x1, g), at(xhat["ln1"], g), [("T_L1" + str(T - 1), g - 1)])],
            9: [lambda g: transposed("L1", g, at(xhat["ln1"], g), ("norm_ln1", g), at(xT_hi["L1"], g),
                                     at(xT_lo["L1"], g), ("Q_L1v", g - 1))],
            10: [lambda g: queries("L1a", "L1", g, at(xT_hi["L1"], g), at(xT_lo["L1"], g)),
                 lambda g: queries("L1v", "L1", g, at(xT_hi["L1"], g), at(xT_lo["L1"], g))],
            11: [lambda g: pe.wait("t_chat", g), lambda g: open_scores("L1a", g, at(keysT["L1a"], g)),
                 lambda g: pe.wait("t_vhat", g), lambda g: open_scores("L1v", g, at(keysT["L1v"], g)),
                 lambda g: softmax("L1a", g, banks_of["L1a", g], "PT_L1a"),
                 lambda g: softmax("L1v", g, banks_of["L1v", g], "PT_L1v")],
            13: [keys_L2, lambda g: prob_transposed("L1a", g, act), lambda g: prob_transposed("L1v", g, act)],
            14: [lambda g: attended("L1a", g, at(keys["L1a"], g)), lambda g: attended("L1v", g, at(keys["L1v"], g))],
            15: [lambda g: project("L1", "L1", g, ["L1a", "L1v"], at(x1, g), at(x2, g),
                                   [("norm_lnf", g - 1), ("out_fc0", g - 1), (f"out_fc{OUT_BANKS - 1}", g - 1)])],
            16: [lambda g: norm_stats("lnf", g, at(x2, g), EPS_L1, written("L1"))],
            17: [lambda g: norm_apply("lnf", g, at(x2, g), at(xhat["lnf"], g), [("T_fc" + str(T - 1), g - 1)])],
            18: [lambda g: transposed("fc", g, at(xhat["lnf"], g), ("norm_lnf", g), at(xT_hi["fc"], g),
                                      at(xT_lo["fc"], g), ("OUT_fc", g - 1))],
            19: [project_fc],
            20: [lambda g: pe.wait("out_fc0", g),
                 lambda g: transposed("L2", g, at(x3, g), (f"out_fc{OUT_BANKS - 1}", g), at(xT2, g), None,
                                      ("S_L2", g - 1))],
            21: [lambda g: banks_of.update({("L2", g): scores_L2(g)}),
                 lambda g: softmax("L2", g, banks_of["L2", g], "OUT_L2")],
            23: [attend_L2],
            24: [lambda g: norm_stats("ln2", g, at(x4, g), EPS_L2, written("L2"))],
            25: [lambda g: norm_apply("ln2", g, at(x4, g), at(xhat["ln2"], g),
                                      [("T_L3" + str(T - 1), g - 1), ("x_res", g - 1)]), gamma_residual],
            26: [lambda g: transposed("L3", g, at(xhat["ln2"], g), ("norm_ln2", g), at(xT_hi["L3"], g),
                                      at(xT_lo["L3"], g), ("Q_L3", g - 1))],
            27: [lambda g: queries("L3", "L3", g, at(xT_hi["L3"], g), at(xT_lo["L3"], g))],
            28: [lambda g: open_scores("L3", g, at(ctxT, g)),
                 lambda g: softmax("L3", g, banks_of["L3", g], "PT_L3")],
            30: [lambda g: prob_transposed("L3", g, act)],
            31: [lambda g: attended("L3", g, at(ctx_in, g))],
            32: [lambda g: dve.wait("x_res", g),
                 lambda g: project("L3", "L3", g, ["L3"], at(x_res, g), at(y, g), [(f"stored{(g - 1) % 2}", g - 1)]),
                 store],
        }

        def ready_prep():
            marks.value["prep_v", "all"] = marks.value["prep_v", chain[0]]
            for q in (pe, act, pool):
                q.wait("prep_v", "all")

        def prep_first():
            prep_L0()
            pe.wait("constants")
            ready_prep()

        def prep_second():
            prep_L2()
            prep_L1()
            pe.wait("w_Wv2")
            ready_prep()

        def prep_third():
            prep_fc()
            prep_L3()
            ready_prep()

        first, last = min(plan), max(plan)
        constants()
        load_weights("L0")
        load(cols[:], ins["cols"].rearrange("p (n t) -> p n t", t=T), "vectors")
        load(rows[:], ins["rows"].rearrange("(o n) d -> o n d", o=1).to_broadcast([P, len(ROWS), D]), "vectors")
        preps = {-1: prep_first, 1: prep_second, 5: prep_third}
        for now in range(first, (GROUPS - 1) * LEAD + last + 1):
            if now in preps:
                preps[now]()
            for g in range(GROUPS):
                for step in plan.get(now - g * LEAD, []):
                    step(g)
                if g == 0 and now == first:
                    for a in ("L2", "L1a", "L1v", "L3"):
                        load_weights(a)
                    load(Wv2[:], ins["L2_Wv"], "w_Wv2")
                    load(fcW[:], ins["fc_W"].rearrange("(t p) n -> p t n", p=P), "w_fc")
        for n in range(2):
            sp.wait(f"stored{n}", GROUPS - 2 + n)

        block = stack.enter_context(nc.Block())
        block.tensor(pe.play)
        block.scalar(act.play)
        block.vector(dve.play)
        block.gpsimd(pool.play)
        block.sync(sp.play)


def layout(inputs):
    import numpy as np

    def name(a, what):
        layer, side = a[:2], a[2:]
        return f"{layer}_xattn_{side + '_' if side else ''}{what}"

    arrays = {"x": inputs["x"], "ctx": inputs["ctx_512"], "side": inputs["fside_BxSxS_0"]}
    for a in ATTENTIONS + ("L2",):
        arrays[f"{a}_WqT"] = inputs[name(a, "Wq")].T
        arrays[f"{a}_WkT"] = inputs[name(a, "Wk")].T
        if a != "L2":
            arrays[f"{a}_WvT"] = inputs[name(a, "Wv")].T
            arrays[f"{a}_Wo"] = inputs[name(a, "Wo")]
    arrays["L2_Wv"] = inputs["L2_xattn_Wv"]
    arrays["fc_W"] = inputs["L1_xattn_fc_W"]
    vectors = {"fc_g": "L1_xattn_ln_g", "fc_b": "L1_xattn_ln_b", "fc_bias": "L1_xattn_fc_b", "L2_bk": "L2_xattn_bk",
               "L2_bv": "L2_xattn_bv", "L3_g1": "L2_xattn_gamma", "L3_b1": "L2_xattn_beta"}
    for a in ATTENTIONS:
        for b in ("bq", "bv", "bo"):
            vectors[f"{a}_{b}"] = name(a, b)
    for a in ("L1a", "L1v"):
        for n in (1, 2):
            vectors[f"{a}_g{n}"] = name(a, f"ln{n}_g")
            vectors[f"{a}_b{n}"] = name(a, f"ln{n}_b")

    def padded(n):
        vector = inputs[vectors[n]]
        return np.concatenate([vector, np.zeros(D - vector.shape[0], vector.dtype)])

    arrays["cols"] = np.stack([padded(n).reshape(T, P) for n in COLS]).transpose(2, 0, 1).reshape(P, len(COLS) * T)
    arrays["rows"] = np.stack([padded(n) for n in ROWS])
    return {n: np.ascontiguousarray(a) for n, a in arrays.items()}


def kernel(**inputs):
    import numpy as np
    import concourse.bacc as bacc
    from concourse.bass_utils import run_bass_kernel_spmd

    nc = bacc.Bacc("TRN2", target_bir_lowering=False, num_devices=1)
    arrays = layout({n: np.asarray(a) for n, a in inputs.items()})
    ins = {n: nc.dram_tensor(f"in_{n}", a.shape, mybir.dt.from_np(a.dtype), kind="ExternalInput").ap()
           for n, a in arrays.items()}
    out = nc.dram_tensor("out", (BATCH, P, D), F32, kind="ExternalOutput").ap()
    build(nc, ins, out)
    result = run_bass_kernel_spmd(nc, [{f"in_{n}": a for n, a in arrays.items()}], core_ids=[0])
    return result.results[0]["out"]
```

```python
from contextlib import ExitStack

import concourse.bass as bass
from concourse import mybir

F32 = mybir.dt.float32
F32R = mybir.dt.float32r
ALU = mybir.AluOpType
ACT = mybir.ActivationFunctionType
AX = mybir.AxisListType

P = 128
D = 256
T = D // P
BATCH = 64
GROUP = 2
GROUPS = BATCH // GROUP
TOK = GROUP * P
BANKS = 8
PERIOD = 184
STARTS = {"load_x": -100, "load_ctx": -100, "load_side": -100, "T_L0": 26, "stats_keys": 30, "hi_L0": 33,
          "rstd_keys": 47, "lo_L0": 51, "shift_keys": 59, "norm_keys": 62, "Q_L0": 85, "q_L0": 93, "T_ctx": 121,
          "T_keys": 123, "t_ctx": 128, "S_L0": 133, "B2": 137, "t_keys": 145, "b2": 149, "max_L0": 153,
          "exp_L0": 159, "V2": 165, "inv_L0": 170, "v2": 178, "prob_L0": 201, "PT_L0": 212, "pT_L0": 230,
          "O_L0": 236, "oT_hi_L0": 245, "oT_lo_L0": 253, "OUT_L0": 292, "out_L0": 320, "stats_ln1": 328,
          "rstd_ln1": 367, "shift_ln1": 379, "norm_ln1": 383, "T_L1": 396, "hi_L1": 415, "lo_L1": 422, "Q_L1": 431,
          "q_L1": 446, "S_L1": 465, "max_L1": 493, "exp_L1": 501, "inv_L1": 517, "prob_L1": 544, "PT_L1": 560,
          "pT_L1": 566, "O_L1": 595, "oT_hi_L1": 617, "oT_lo_L1": 624, "OUT_L1": 635, "out_L1": 653,
          "stats_lnf": 661, "rstd_lnf": 675, "shift_lnf": 689, "norm_lnf": 692, "T_fc": 710, "hi_fc": 717,
          "lo_fc": 734, "OUT_fc": 743, "out_fc": 760, "T_L2": 771, "hi_L2": 779, "S_L2": 786, "max_L2": 801,
          "exp_L2": 807, "inv_L2": 816, "prob_L2": 821, "OUT_L2": 833, "out_L2": 847, "stats_ln2": 856,
          "rstd_ln2": 870, "shift_ln2": 885, "norm_ln2": 890, "T_L3": 904, "x_res": 908, "hi_L3": 915,
          "lo_L3": 923, "Q_L3": 943, "q_L3": 952, "S_L3": 958, "max_L3": 967, "exp_L3": 972, "inv_L3": 982,
          "prob_L3": 998, "PT_L3": 1012, "pT_L3": 1017, "O_L3": 1027, "oT_hi_L3": 1037, "oT_lo_L3": 1042,
          "OUT_L3": 1049, "out_L3": 1069, "store": 1078}
PREPARATIONS = {"load_first": -110, "constants": -109, "load_rest": 2, "keys_L0": 5, "products_L0": 6,
                "vectors_L0": 7, "L2": 10, "keys_L1": 30, "products_L1": 50, "vectors_L1": 90, "keys_L3": 110,
                "fc": 120, "products_L3": 140, "vectors_L3": 160}
COPIES = {"x_in": 3, "ctx_in": 7, "side_in": 2, "ctxT": 5, "keys": 4, "keysT": 3, "V2": 4, "B2": 4, "x1": 3,
          "x2": 1, "xhat_ln1": 1, "xhat_lnf": 1, "xhat_ln2": 1, "x3": 1, "x4": 1, "x_res": 2, "y": 2,
          "xT_hi_L0": 1, "xT_lo_L0": 1, "prob_L0": 1, "neg_max_L0": 1, "total_L0": 1, "inv_total_L0": 1,
          "qT_L0": 1, "probT_L0": 1, "oT_hi_L0": 1, "oT_lo_L0": 1, "xT_hi_L1": 1, "xT_lo_L1": 1, "prob_L1": 1,
          "neg_max_L1": 1, "total_L1": 1, "inv_total_L1": 1, "qT_L1": 1, "probT_L1": 1, "oT_hi_L1": 1,
          "oT_lo_L1": 1, "xT_hi_fc": 1, "xT_lo_fc": 1, "xT_hi_L2": 1, "prob_L2": 1, "neg_max_L2": 1, "total_L2": 1,
          "inv_total_L2": 1, "xT_hi_L3": 1, "xT_lo_L3": 1, "prob_L3": 1, "neg_max_L3": 1, "total_L3": 1,
          "inv_total_L3": 1, "qT_L3": 1, "probT_L3": 1, "oT_hi_L3": 1, "oT_lo_L3": 1, "stats_keys": 1,
          "mean_var_keys": 1, "var_eps_keys": 1, "rstd_keys": 1, "shift_keys": 1, "stats_ln1": 1,
          "mean_var_ln1": 1, "var_eps_ln1": 1, "rstd_ln1": 1, "shift_ln1": 1, "stats_lnf": 1, "mean_var_lnf": 1,
          "var_eps_lnf": 1, "rstd_lnf": 1, "shift_lnf": 1, "stats_ln2": 1, "mean_var_ln2": 1, "var_eps_ln2": 1,
          "rstd_ln2": 1, "shift_ln2": 1}
ON_VECTOR = ()

SCALE = float(D) ** -0.5
EPS_L1 = 1e-5
EPS_L2 = 1e-6

LAYERS = {"L0": ["L0"], "L1": ["L1a", "L1v"], "L3": ["L3"]}
ATTENTIONS = ["L0", "L1a", "L1v", "L3"]
COLS = ["L0_bq", "L0_bv", "L1a_bq", "L1a_bv", "L1a_g1", "L1a_b1", "L1v_bq", "L1v_bv", "L1v_g1", "L1v_b1",
        "L3_bq", "L3_bv", "L3_g1", "L3_b1", "L2_bk", "fc_g", "fc_b", "L1a_b2", "L1v_b2", "L1a_g2", "L1v_g2"]
ROWS = ["L0_bo", "L1a_bo", "L1v_bo", "L3_bo", "fc_bias", "L2_bv", "L3_b1", "L3_g1", "L1a_g2", "L1v_g2"]


class Marks:

    def __init__(self, nc, stack):
        self.nc, self.stack, self.sems, self.count, self.value, self.order = nc, stack, {}, {}, {}, {}

    NEVER = 1 << 30

    def raised(self, counter, step, group, increment):
        if counter not in self.sems:
            self.sems[counter] = self.stack.enter_context(self.nc.semaphore("s_" + counter))
            self.count[counter] = 0
        self.count[counter] += increment
        self.value[step, group] = counter, self.count[counter]
        self.order[step, group] = len(self.order)
        return self.sems[counter]

    def also(self, name, mark):
        self.value[name], self.order[name] = self.value[mark], self.order[mark]


class Queue:

    def __init__(self, marks, name):
        self.marks, self.name, self.items, self.reached = marks, name, [], {}

    def wait(self, step, group=0):
        if isinstance(group, int) and group < 0:
            return
        counter, value = self.marks.value[step, group]
        if self.reached.get(counter, 0) < value:
            self.reached[counter] = value
            sem = self.marks.sems[counter]
            self.items.append(lambda e: e.wait_ge(sem, value))

    def op(self, method, *args, done=None, **kw):
        if done is None:
            self.items.append(lambda e: method(*args, **kw))
        else:
            sem = self.marks.raised(self.name, *done, 1)
            self.items.append(lambda e: method(*args, **kw).then_inc(sem, 1))

    def dma(self, method, dst, src, done):
        sem = self.marks.raised(done[0], *done, 16)
        self.items.append(lambda e: method(dst, src).then_inc(sem, 16))

    def play(self, e):
        for item in self.items:
            item(e)


class Banks:

    def __init__(self, banks, pe, marks):
        self.banks, self.pe, self.marks = banks, pe, marks
        self.readers = [None] * len(banks)

    def take(self, step, group=0):
        order = [-1 if r is None else self.marks.order.get(r, self.marks.NEVER) for r in self.readers]
        n = order.index(min(order))
        assert order[n] < self.marks.NEVER, f"no bank for {step} {group}"
        if self.readers[n]:
            self.pe.wait(*self.readers[n])
        self.readers[n] = step, group
        return self.banks[n]


def build(nc, ins, out):
    stack = ExitStack()
    with stack:
        marks = Marks(nc, stack)
        pe, act, dve, pool, sp = (Queue(marks, n) for n in ("pe", "act", "dve", "pool", "sp"))
        mm, tr = nc.tensor.matmul, nc.tensor.transpose

        def sb(name, shape, dtype=F32, where=stack):
            return where.enter_context(nc.sbuf_tensor(name, shape, dtype))

        def ring(name, copies, shape, dtype=F32):
            return [sb(f"{name}_{i}", shape, dtype) for i in range(copies)]

        banks = Banks([stack.enter_context(nc.psum_tensor(f"bank{i}", [P, 512], F32)) for i in range(BANKS)], pe, marks)

        ident = sb("ident", [P, P])
        minus_half = sb("minus_half", [P, 2 * GROUP])
        ones_r = sb("ones_r", [P, P], F32R)
        ones_row = sb("ones_row", [1, P])
        cols = sb("cols", [P, len(COLS), T])
        scaled_cols = sb("scaled_cols", [P, len(COLS), T])
        gamma_row = sb("gamma_row", [P, D])
        M_hi = {a: sb(f"M_hi_{a}", [P, T, P], F32R) for a in ATTENTIONS}
        M_lo = {a: sb(f"M_lo_{a}", [P, T, P], F32R) for a in ATTENTIONS}
        N_hi = {a: sb(f"N_hi_{a}", [P, D], F32R) for a in ATTENTIONS}
        N_lo = {a: sb(f"N_lo_{a}", [P, D], F32R) for a in ATTENTIONS}
        m_col = {a: sb(f"m_{a}", [P, 1]) for a in ATTENTIONS}
        F_hi, F_lo = sb("F_hi", [P, T, D], F32R), sb("F_lo", [P, T, D], F32R)
        M2T, Wv2, k_bias2 = sb("M2T", [P, D]), sb("Wv2", [P, D]), sb("k_bias2", [P, T])
        bias_hl = {k: sb(f"bias_{k}", [P, D], F32R) for k in ("L0", "L1", "fc", "L2v", "L3")}

        def ring(name, shape, dtype=F32):
            return [sb(f"{name}_{i}", shape, dtype) for i in range(COPIES[name])]

        A = {k: len(LAYERS.get(k, [k])) for k in ("L0", "L1", "L2", "L3")}
        x_in = ring("x_in", [P, GROUP, D])
        ctx_in = ring("ctx_in", [P, GROUP, P])
        side_in = ring("side_in", [P, GROUP, P])
        ctxT = ring("ctxT", [P, TOK])
        keys = ring("keys", [P, A["L1"] * GROUP, P])
        keysT = ring("keysT", [P, A["L1"] * TOK])
        V2 = ring("V2", [P, GROUP, D])
        B2 = ring("B2", [P, T, TOK])
        x1 = ring("x1", [P, GROUP, D])
        x2 = ring("x2", [P, GROUP, D])
        xhat = {"ln1": ring("xhat_ln1", [P, GROUP, D]), "lnf": ring("xhat_lnf", [P, GROUP, D])}
        xT_hi, xT_lo, qT, prob, probT, oT_hi, oT_lo = ({} for _ in range(7))

        def layer_buffers(k):
            xT_hi[k] = ring(f"xT_hi_{k}", [P, T, TOK], F32 if k == "L2" else F32R)
            if k != "L2":
                xT_lo[k] = ring(f"xT_lo_{k}", [P, T, TOK], F32R)
            if k != "fc":
                prob[k] = ring(f"prob_{k}", [P, A[k] * GROUP, P])
            if k in LAYERS:
                qT[k] = ring(f"qT_{k}", [P, A[k] * TOK])
                probT[k] = ring(f"probT_{k}", [P, A[k] * TOK])
                oT_hi[k] = ring(f"oT_hi_{k}", [P, A[k] * TOK], F32R)
                oT_lo[k] = ring(f"oT_lo_{k}", [P, A[k] * TOK], F32R)

        for k in ("L0", "L1", "fc"):
            layer_buffers(k)
        stats, mean_var, var_eps, rstd, shift = ({} for _ in range(5))
        for k, n in {"keys": A["L1"] * GROUP, "ln1": GROUP, "lnf": GROUP, "ln2": GROUP}.items():
            stats[k] = ring(f"stats_{k}", [P, n, 6])
            mean_var[k] = ring(f"mean_var_{k}", [P, n, 2])
            var_eps[k] = ring(f"var_eps_{k}", [P, n])
            rstd[k] = ring(f"rstd_{k}", [P, n])
            shift[k] = ring(f"shift_{k}", [P, n])
        neg_max, total, inv_total = {}, {}, {}
        for k in A:
            neg_max[k] = ring(f"neg_max_{k}", [P, A[k] * GROUP])
            total[k] = ring(f"total_{k}", [P, A[k] * GROUP])
            inv_total[k] = ring(f"inv_total_{k}", [P, A[k] * GROUP])

        stage, temp = {}, {}
        with ExitStack() as staging:
            for a in ATTENTIONS + ["L2"]:
                stage[a] = {"WqT": sb(f"WqT_{a}", [P, T, D], where=staging), "WkT": sb(f"WkT_{a}", [P, T, P], where=staging)}
                if a != "L2":
                    stage[a]["WvT"] = sb(f"WvT_{a}", [P, T, P], where=staging)
                    stage[a]["Wo"] = sb(f"Wo_{a}", [P, T, D], where=staging)
            fcW = sb("fcW", [P, T, D], where=staging)
            rows = sb("rows", [1, len(ROWS), D], where=staging)
            for a in ATTENTIONS + ["fc"]:
                temp[a] = {"bv": sb(f"rep_bv_{a}", [P, T, P], where=staging), "hi": sb(f"bias_hi_{a}", [P, D], F32R, where=staging)}
            for a in ("L1a", "L1v"):
                temp[a]["N0"] = sb(f"N0_{a}", [P, D], where=staging)
                temp[a]["b2"] = sb(f"rep_b2_{a}", [P, P], where=staging)
            for a in ("L1a", "L1v", "L3"):
                temp[a]["M0"] = sb(f"M0_{a}", [P, T, P], where=staging)
            temp["L2v"] = {"hi": sb("bias_hi_L2v", [P, D], F32R, where=staging)}
        x3 = ring("x3", [P, GROUP, D])
        x4 = ring("x4", [P, GROUP, D])
        xhat["ln2"] = ring("xhat_ln2", [P, GROUP, D])
        layer_buffers("L2")
        layer_buffers("L3")
        x_res = ring("x_res", [P, GROUP, D])
        y = ring("y", [P, GROUP, D])

        def at(buffers, g):
            return buffers[g % len(buffers)]

        def f32(tile):
            return tile[:].bitcast(F32)

        v = nc.vector
        LN = ("L1a", "L1v", "L3")
        LN_KEYS = ("L1a", "L1v")

        def col(name, t=0, of=cols):
            n = COLS.index(name)
            return of[:, n, t:t + 1]

        def row(name, width=D):
            return rows[0:1, ROWS.index(name), 0:width]

        def load(dst, src, stream):
            sp.dma(nc.sync.dma_start, dst, src, done=(stream, 0))

        def load_weights(a):
            for w in stage[a]:
                load(stage[a][w][:], ins[f"{a}_{w}"].rearrange("(t p) n -> p t n", p=P), f"w_{a}")

        def load_first():
            load(cols[:], ins["cols"].rearrange("p (n t) -> p n t", t=T), "vectors")
            load(rows[:], ins["rows"].rearrange("(o n) d -> o n d", o=1), "vectors")
            load_weights("L0")

        def load_rest():
            load_weights("L1a")
            load_weights("L1v")
            load_weights("L2")
            load(Wv2[:], ins["L2_Wv"], "w_L2")
            load(fcW[:], ins["fc_W"].rearrange("(t p) n -> p t n", p=P), "w_fc")
            load_weights("L3")

        def constants():
            pool.op(nc.gpsimd.memset, ident[:], 0.0, done=("zeroed", 0))
            pool.wait("zeroed")
            pool.op(nc.gpsimd.affine_select, out=ident[:], in_=ident[:], compare_op=ALU.not_equal, fill=1.0,
                    base=0, pattern=[[-1, P]], channel_multiplier=1, done=("ident", 0))
            pool.op(nc.gpsimd.memset, minus_half[:], -0.5)
            pool.op(nc.gpsimd.memset, ones_r[:].bitcast(F32), 1.0)
            pool.op(nc.gpsimd.memset, ones_row[:], 1.0)
            for k in bias_hl:
                pool.op(nc.gpsimd.memset, bias_hl[k][:].bitcast(F32), 0.0, done=("constants", 0))
            pe.wait("constants")
            dve.wait("constants")
            act.wait("constants")
            dve.wait("vectors")
            dve.op(v.tensor_scalar, scaled_cols[:].rearrange("p n t -> p (n t)"), cols[:].rearrange("p n t -> p (n t)"),
                   SCALE, None, ALU.mult, done=("scaled", 0))
            for q in (pe, act, pool):
                q.wait("vectors")
            pe.wait("scaled")
            act.wait("scaled")
            dve.wait("scaled")

        def replicate(a, name, what, n):
            for t in range(n):
                pool.op(nc.gpsimd.tensor_copy, temp[a][what][:, t, :] if n > 1 else temp[a][what][:],
                        col(name, t).to_broadcast([P, P]), done=(f"rep_{what}", a))

        def bias_row(key, a, bank, produced):
            act.wait(*produced)
            dve.wait(*produced)
            hi = temp[a]["hi"]
            act.op(nc.scalar.activation, hi[:], bank[:, 0:D], ACT.Copy, done=("bias_hi", key))
            act.op(nc.scalar.activation, bias_hl[key][0:1, :], bank[0:1, 0:D], ACT.Copy, done=("bias_hl", key))
            dve.wait("bias_hi", key)
            dve.op(v.tensor_tensor, bias_hl[key][32:33, :], bank[32:33, 0:D], hi[32:33, :].bitcast(F32), ALU.subtract,
                   done=("bias_lo", key))

        def split_product(hi, lo, bank, produced, name, a, scales):
            width = D // len(scales)
            act.wait(*produced)
            dve.wait(*produced)
            for i, scale in enumerate(scales):
                s = slice(i * width, (i + 1) * width)
                act.op(nc.scalar.activation, hi[:, s], bank[:, s], ACT.Copy, scale=scale, done=(f"{name}_hi", a))
            dve.wait(f"{name}_hi", a)
            for i, scale in enumerate(scales):
                s = slice(i * width, (i + 1) * width)
                dve.op(v.scalar_tensor_tensor, out=lo[:, s], in0=bank[:, s], scalar=scale, in1=hi[:, s].bitcast(F32),
                       op0=ALU.mult, op1=ALU.subtract, done=(f"{name}_lo", a))

        def prep_keys(a):
            w = stage[a]
            replicate(a, f"{a}_bv", "bv", T)
            if a in LN_KEYS:
                replicate(a, f"{a}_b2", "b2", 1)
                bank = banks.take("WkT", a)
                pe.op(mm, bank[:, 0:P], ones_row[:], row(f"{a}_g2", P), start=True, stop=True, done=("gain", a))
                dve.wait("gain", a)
                dve.wait(f"w_{a}")
                for t in range(T):
                    dve.op(v.tensor_tensor, w["WkT"][:, t, :], w["WkT"][:, t, :], bank[:, 0:P], ALU.mult, done=("WkT", a))

        def prep_products(a):
            w = stage[a]
            pe.wait(f"w_{a}")
            if a in LN_KEYS:
                pe.wait("WkT", a)
            bank_M, bank_N = banks.take("M_done", a), None
            for e in range(T):
                for h in range(T):
                    pe.op(mm, bank_M[:, e * P:(e + 1) * P], w["WqT"][:, h, e * P:(e + 1) * P], w["WkT"][:, h, :],
                          start=h == 0, stop=h == T - 1, done=("prod_M", a))
            bank_N = banks.take("N_done", a)
            for h in range(T):
                pe.op(mm, bank_N[:, 0:D], w["WvT"][:, h, :], w["Wo"][:, h, :], start=h == 0, stop=h == T - 1,
                      done=("prod_N", a))
            gains = [col(f"{a}_g1", t, scaled_cols) for t in range(T)] if a in LN else [SCALE]
            M_flat = [x[a][:].rearrange("p t d -> p (t d)") for x in (M_hi, M_lo)]
            act.wait("prod_M", a)
            if a in LN:
                act.op(nc.scalar.activation, temp[a]["M0"][:].rearrange("p t d -> p (t d)"), bank_M[:, 0:D], ACT.Copy,
                       done=("M0", a))
            split_product(*M_flat, bank_M, ("prod_M", a), "M", a, gains)
            marks.also(("M_done", a), ("M_lo", a))
            act.wait("prod_N", a)
            if a in LN_KEYS:
                act.op(nc.scalar.activation, temp[a]["N0"][:], bank_N[:, 0:D], ACT.Copy, done=("N0", a))
            split_product(N_hi[a], N_lo[a], bank_N, ("prod_N", a), "N", a, [col(f"{a}_g2")] if a in LN_KEYS else [1.0])
            marks.also(("N_done", a), ("N_lo", a))

        def prep_m(a):
            w = stage[a]
            bank = banks.take("m", a)
            terms = [(w["WkT"][:, h, :], col(f"{a}_bq", h, scaled_cols)) for h in range(T)]
            if a in LN:
                pe.wait("M0", a)
                terms += [(temp[a]["M0"][:, e, :], col(f"{a}_b1", e, scaled_cols)) for e in range(T)]
            for n, (stationary, moving) in enumerate(terms):
                pe.op(mm, bank[:, 0:1], stationary, moving, start=n == 0, stop=n == len(terms) - 1, done=("prod_m", a))
            act.wait("prod_m", a)
            act.op(nc.scalar.activation, m_col[a][:], bank[:, 0:1], ACT.Copy, done=("m", a))

        def prep_bias(key, attentions, extra):
            last = attentions[-1]
            bank = banks.take("bias_lo", key)
            terms = []
            for a in attentions:
                pe.wait("rep_bv", a)
                terms += [(temp[a]["bv"][:, h, :], stage[a]["Wo"][:, h, :]) for h in range(T)]
                if a in LN_KEYS:
                    pe.wait("rep_b2", a)
                    pe.wait("N0", a)
                    terms += [(temp[a]["b2"][:], temp[a]["N0"][:])]
            terms += [(ones_row[:], row(r)) for r in extra]
            for n, (stationary, moving) in enumerate(terms):
                pe.op(mm, bank[:, 0:D], stationary, moving, start=n == 0, stop=n == len(terms) - 1, done=("prod_n", key))
            bias_row(key, last, bank, ("prod_n", key))

        def prep_fc():
            replicate("fc", "fc_b", "bv", T)
            pe.wait("w_fc")
            pe.wait("rep_bv", "fc")
            bank = banks.take("bias_lo", "fc")
            terms = [(temp["fc"]["bv"][:, t, :], fcW[:, t, :]) for t in range(T)] + [(ones_row[:], row("fc_bias"))]
            for n, (stationary, moving) in enumerate(terms):
                pe.op(mm, bank[:, 0:D], stationary, moving, start=n == 0, stop=n == len(terms) - 1, done=("prod_n", "fc"))
            act.wait("w_fc")
            dve.wait("w_fc")
            for t in range(T):
                act.op(nc.scalar.activation, F_hi[:, t, :], fcW[:, t, :], ACT.Copy, scale=col("fc_g", t), done=("F_hi", 0))
            dve.wait("F_hi")
            for t in range(T):
                dve.op(v.scalar_tensor_tensor, out=F_lo[:, t, :], in0=fcW[:, t, :], scalar=col("fc_g", t),
                       in1=F_hi[:, t, :].bitcast(F32), op0=ALU.mult, op1=ALU.subtract, done=("F_lo", 0))
            bias_row("fc", "fc", bank, ("prod_n", "fc"))

        def prep_L2():
            w = stage["L2"]
            pe.wait("w_L2")
            bank = banks.take("M2T")
            for h in range(T):
                pe.op(mm, bank[:, 0:D], w["WkT"][:, h, :], w["WqT"][:, h, :], start=h == 0, stop=h == T - 1,
                      done=("prod_M", "L2"))
            act.wait("prod_M", "L2")
            act.op(nc.scalar.activation, M2T[:], bank[:, 0:D], ACT.Copy, scale=SCALE, done=("M2T", 0))
            bank = banks.take("k_bias2")
            for e in range(T):
                for h in range(T):
                    pe.op(mm, bank[:, e:e + 1], w["WqT"][:, h, e * P:(e + 1) * P], col("L2_bk", h, scaled_cols),
                          start=h == 0, stop=h == T - 1, done=("prod_m", "L2"))
            act.wait("prod_m", "L2")
            act.op(nc.scalar.activation, k_bias2[:], bank[:, 0:T], ACT.Copy, done=("k_bias2", 0))
            bank = banks.take("bias_lo", "L2v")
            pe.op(mm, bank[:, 0:D], ones_row[:], row("L2_bv"), start=True, stop=True, done=("prod_n", "L2"))
            bias_row("L2v", "L2v", bank, ("prod_n", "L2"))

        def prep_gamma():
            bank = banks.take("gamma_row")
            pe.op(mm, bank[:, 0:D], ones_row[:], row("L3_g1"), start=True, stop=True, done=("spread", 0))
            act.wait("spread")
            act.op(nc.scalar.activation, gamma_row[:], bank[:, 0:D], ACT.Copy, done=("gamma_row", 0))

        preparations = {
            "load_first": load_first, "constants": constants, "load_rest": load_rest,
            "keys_L0": lambda: prep_keys("L0"), "products_L0": lambda: prep_products("L0"),
            "vectors_L0": lambda: (prep_m("L0"), prep_bias("L0", ["L0"], ["L0_bo"])),
            "keys_L1": lambda: (prep_keys("L1a"), prep_keys("L1v")),
            "products_L1": lambda: (prep_products("L1a"), prep_products("L1v")),
            "vectors_L1": lambda: (prep_m("L1a"), prep_m("L1v"), prep_bias("L1", ["L1a", "L1v"], ["L1a_bo", "L1v_bo"])),
            "L2": prep_L2, "fc": prep_fc,
            "keys_L3": lambda: prep_keys("L3"), "products_L3": lambda: prep_products("L3"),
            "vectors_L3": lambda: (prep_m("L3"), prep_bias("L3", ["L3"], ["L3_bo", "L3_b1"]), prep_gamma()),
        }

        steps = {}
        held = {}

        def step(name):
            def keep(function):
                steps[name] = function
                return function
            return keep

        def evacuate(name, g, pieces, last=True):
            for i, (dst, src, bias) in enumerate(pieces):
                done = (name, g) if i == len(pieces) - 1 else None
                if name in ON_VECTOR and bias is None:
                    dve.op(v.tensor_copy, dst, src, done=done)
                elif name in ON_VECTOR:
                    dve.op(v.tensor_scalar, dst, src, bias, None, ALU.add, done=done)
                elif bias is None:
                    act.op(nc.scalar.activation, dst, src, ACT.Copy, done=done)
                else:
                    act.op(nc.scalar.activation, dst, src, ACT.Identity, bias=bias, done=done)

        def engine_of(name):
            return dve if name in ON_VECTOR else act

        def blocks(bank, n):
            return [bank[:, b * P:(b + 1) * P] for b in range(n)]

        def loaded(what, ring, g):
            return f"{what}{g % len(ring)}"

        def split_evacuation(produced, hi_step, lo_step, hi, lo, freed_by):
            @step(hi_step)
            def _(g):
                engine = engine_of(hi_step)
                engine.wait(produced, g)
                engine.wait(freed_by, g - len(hi))
                evacuate(hi_step, g, [(flat(at(hi, g)), flat_like(held[produced, g], hi), None)])

            @step(lo_step)
            def _(g):
                dve.wait(hi_step, g)
                dve.wait(freed_by, g - len(lo))
                dve.op(v.tensor_tensor, flat(at(lo, g)), flat_like(held.pop((produced, g)), hi),
                       flat(at(hi, g)).bitcast(F32), ALU.subtract, done=(lo_step, g))

        def flat(tile):
            return tile[:] if len(tile.shape) == 2 else tile[:].rearrange("p a n -> p (a n)")

        def flat_like(bank, ring):
            n = 1
            for extent in ring[0].shape[1:]:
                n *= extent
            return bank[:, 0:n]

        def transposed(k, src, after, freed_by):
            @step(f"T_{k}")
            def _(g):
                pe.wait(after(g), g)
                last = f"hi_{k}" if k == "L2" else f"lo_{k}"
                bank = held[f"T_{k}", g] = banks.take(last, g)
                for t in range(T):
                    for b in range(GROUP):
                        n = t * GROUP + b
                        pe.op(tr, bank[:, n * P:(n + 1) * P], at(src, g)[:, b, t * P:(t + 1) * P], ident[:],
                              done=(f"T_{k}", g) if n == T * GROUP - 1 else None)

            if k != "L2":
                split_evacuation(f"T_{k}", f"hi_{k}", f"lo_{k}", xT_hi[k], xT_lo[k], freed_by)
            else:
                @step(f"hi_{k}")
                def _(g):
                    engine = engine_of(f"hi_{k}")
                    engine.wait(f"T_{k}", g)
                    engine.wait(freed_by, g - len(xT_hi[k]))
                    evacuate(f"hi_{k}", g, [(flat(at(xT_hi[k], g)), held.pop((f"T_{k}", g))[:], None)])

        def blocks_transposed(produce, evacuated, n, src, after, dst, freed_by):
            @step(produce)
            def _(g):
                pe.wait(after(g), g)
                bank = held[produce, g] = banks.take(evacuated, g)
                for b, block in enumerate(blocks(bank, n)):
                    pe.op(tr, block, at(src, g)[:, b, :], ident[:], done=(produce, g) if b == n - 1 else None)

            @step(evacuated)
            def _(g):
                engine = engine_of(evacuated)
                engine.wait(produce, g)
                engine.wait(freed_by, g - len(dst))
                evacuate(evacuated, g, [(at(dst, g)[:], held.pop((produce, g))[:, 0:n * P], None)])

        def queries_and_scores(k, kT, after):
            @step(f"Q_{k}")
            def _(g):
                bank = held[f"Q_{k}", g] = banks.take(f"q_{k}", g)
                pe.wait(f"lo_{k}", g)
                for a in LAYERS[k]:
                    pe.wait("M_lo", a)
                hi, lo = at(xT_hi[k], g), at(xT_lo[k], g)
                for i, a in enumerate(LAYERS[k]):
                    passes = [(w, x, t) for t in range(T) for w, x in ((M_hi[a], hi), (M_lo[a], hi), (M_hi[a], lo))]
                    for n, (w, x, t) in enumerate(passes):
                        last = n == len(passes) - 1
                        pe.op(mm, bank[:, i * TOK:(i + 1) * TOK], w[:, t, :], x[:, t, :], start=n == 0, stop=last,
                              done=(f"Q_{k}", g) if last and i == A[k] - 1 else None)

            @step(f"q_{k}")
            def _(g):
                engine = engine_of(f"q_{k}")
                engine.wait(f"Q_{k}", g)
                engine.wait("m", LAYERS[k][-1])
                engine.wait(f"S_{k}", g - len(qT[k]))
                bank = held.pop((f"Q_{k}", g))
                evacuate(f"q_{k}", g, [(at(qT[k], g)[:, i * TOK:(i + 1) * TOK], bank[:, i * TOK:(i + 1) * TOK],
                                        m_col[a][:, 0:1]) for i, a in enumerate(LAYERS[k])])

            @step(f"S_{k}")
            def _(g):
                pe.wait(after, g)
                pe.wait(f"q_{k}", g)
                bank = held[f"S_{k}", g] = banks.take(f"exp_{k}", g)
                n = A[k] * GROUP
                for b, (block, q, c) in enumerate(zip(blocks(bank, n), blocks(at(qT[k], g), n), blocks(at(kT, g), n))):
                    pe.op(mm, block, q, c, start=True, stop=True, done=(f"S_{k}", g) if b == n - 1 else None)

        def softmax(k, freed_by):
            n = A[k] * GROUP

            @step(f"max_{k}")
            def _(g):
                dve.wait(f"S_{k}", g)
                dve.wait(f"exp_{k}", g - len(neg_max[k]))
                dve.op(v.tensor_reduce, at(neg_max[k], g)[:], held[f"S_{k}", g][:, 0:n * P].rearrange("p (b k) -> p b k", k=P),
                       AX.X, ALU.max, negate=True, done=(f"max_{k}", g))

            @step(f"exp_{k}")
            def _(g):
                act.wait(f"max_{k}", g)
                act.wait(freed_by, g - len(prob[k]))
                act.wait(f"inv_{k}", g - len(total[k]))
                for b, block in enumerate(blocks(held.pop((f"S_{k}", g)), n)):
                    act.op(nc.scalar.activation, at(prob[k], g)[:, b, :], block, ACT.Exp,
                           bias=at(neg_max[k], g)[:, b:b + 1], accum_out=at(total[k], g)[:, b:b + 1],
                           done=(f"exp_{k}", g) if b == n - 1 else None)

            @step(f"inv_{k}")
            def _(g):
                dve.wait(f"exp_{k}", g)
                dve.wait(f"prob_{k}", g - len(inv_total[k]))
                dve.op(v.reciprocal, at(inv_total[k], g)[:], at(total[k], g)[:], done=(f"inv_{k}", g))

            @step(f"prob_{k}")
            def _(g):
                pool.wait(f"inv_{k}", g)
                p = at(prob[k], g)
                for b in range(n):
                    pool.op(nc.gpsimd.tensor_scalar, p[:, b, :], p[:, b, :], at(inv_total[k], g)[:, b:b + 1], 1.0,
                            ALU.mult, ALU.mult, done=(f"prob_{k}", g) if b == n - 1 else None)

        def attended(k, natural):
            blocks_transposed(f"PT_{k}", f"pT_{k}", A[k] * GROUP, prob[k], lambda g: f"prob_{k}", probT[k], f"O_{k}")

            @step(f"O_{k}")
            def _(g):
                pe.wait(f"pT_{k}", g)
                bank = held[f"O_{k}", g] = banks.take(f"oT_lo_{k}", g)
                n = A[k] * GROUP
                for b, (block, p) in enumerate(zip(blocks(bank, n), blocks(at(probT[k], g), n))):
                    pe.op(mm, block, at(natural, g)[:, b, :], p, start=True, stop=True,
                          done=(f"O_{k}", g) if b == n - 1 else None)

            split_evacuation(f"O_{k}", f"oT_hi_{k}", f"oT_lo_{k}", oT_hi[k], oT_lo[k], f"OUT_{k}")

        def wide_bias(key, bank):
            pe.wait("bias_hl", key)
            pe.wait("bias_lo", key)
            pe.op(mm, bank[:], ones_r[:], bias_hl[key][:].unsqueeze(1).to_broadcast([P, GROUP, D]),
                  start=True, stop=False)

        def project(k):
            @step(f"OUT_{k}")
            def _(g):
                bank = held[f"OUT_{k}", g] = banks.take(f"out_{k}", g)
                for a in LAYERS[k]:
                    pe.wait("N_lo", a)
                wide_bias(k, bank)
                pe.wait(f"oT_lo_{k}", g)
                hi, lo = at(oT_hi[k], g), at(oT_lo[k], g)
                products = []
                for b in range(GROUP):
                    for i, a in enumerate(LAYERS[k]):
                        s = slice((i * GROUP + b) * P, (i * GROUP + b + 1) * P)
                        products += [(b, hi[:, s], N_hi[a][:]), (b, hi[:, s], N_lo[a][:]), (b, lo[:, s], N_hi[a][:])]
                accumulate(f"OUT_{k}", g, bank, products)

        def accumulate(name, g, bank, products):
            for n, (b, stationary, moving) in enumerate(products):
                last = n == len(products) - 1
                pe.op(mm, bank[:, b * D:(b + 1) * D], stationary, moving, start=False, stop=last,
                      done=(name, g) if last else None)

        def residual(k, add, after, dst, freed_by):
            @step(f"out_{k}")
            def _(g):
                dve.wait(f"OUT_{k}", g)
                dve.wait(after(g), g)
                for r in freed_by(g - len(dst)):
                    dve.wait(r, g - len(dst))
                dve.op(v.tensor_tensor, flat(at(dst, g)), held.pop((f"OUT_{k}", g))[:], flat(at(add, g)), ALU.add,
                       done=(f"out_{k}", g))

        def layernorm(k, sources, after, dst, eps, freed_by):
            tiles = [(ring, b) for ring in sources for b in range(GROUP)]

            @step(f"stats_{k}")
            def _(g):
                st, mv = at(stats[k], g), at(mean_var[k], g)
                for w in after(g):
                    dve.wait(w, g)
                dve.wait(f"mv_{k}", g - len(stats[k]))
                for n, (src, b) in enumerate(tiles):
                    dve.op(v.bn_stats, st[:, n, :], at(src, g)[:, b, :], done=(f"st_{k}", g) if n == len(tiles) - 1 else None)
                dve.wait(f"st_{k}", g)
                dve.wait(f"shift_{k}", g - len(mean_var[k]))
                for n in range(len(tiles)):
                    dve.op(v.bn_aggr, mv[:, n, :], st[:, n, :], done=(f"mv_{k}", g) if n == len(tiles) - 1 else None)
                dve.wait(f"mv_{k}", g)
                dve.wait(f"rstd_{k}", g - len(var_eps[k]))
                dve.op(v.tensor_scalar, at(var_eps[k], g)[:], mv[:, :, 1], eps, None, ALU.add, done=(f"ve_{k}", g))

            @step(f"rstd_{k}")
            def _(g):
                pool.wait(f"ve_{k}", g)
                pool.wait("constants")
                pool.wait(f"shift_{k}", g - len(rstd[k]))
                pool.op(nc.gpsimd.tensor_tensor, at(rstd[k], g)[:], at(var_eps[k], g)[:], minus_half[:, 0:len(tiles)],
                        ALU.pow, done=(f"rstd_{k}", g))

            @step(f"shift_{k}")
            def _(g):
                dve.wait(f"rstd_{k}", g)
                dve.wait(f"norm_{k}", g - len(shift[k]))
                dve.op(v.scalar_tensor_tensor, out=at(shift[k], g)[:], in0=at(mean_var[k], g)[:, :, 0], scalar=-1.0,
                       in1=at(rstd[k], g)[:], op0=ALU.mult, op1=ALU.mult, done=(f"shift_{k}", g))

            @step(f"norm_{k}")
            def _(g):
                engine, method = (dve, v.tensor_scalar) if f"norm_{k}" in ON_VECTOR else (pool, nc.gpsimd.tensor_scalar)
                for w in after(g):
                    engine.wait(w, g)
                engine.wait(f"shift_{k}", g)
                for r in freed_by:
                    engine.wait(r, g - len(dst))
                for n, (src, b) in enumerate(tiles):
                    engine.op(method, at(dst, g)[:, n, :], at(src, g)[:, b, :], at(rstd[k], g)[:, n:n + 1],
                              at(shift[k], g)[:, n:n + 1], ALU.mult, ALU.add,
                              done=(f"norm_{k}", g) if n == len(tiles) - 1 else None)

        def seqs(tensor, g):
            return tensor[g * GROUP:(g + 1) * GROUP].rearrange("b p e -> p b e")

        def group_load(what, source, ring, freed_by):
            @step(f"load_{what}")
            def _(g):
                sp.wait(freed_by, g - len(ring))
                sp.dma(nc.sync.dma_start, at(ring, g)[:], seqs(ins[source], g), done=(loaded(what, ring, g), g))

        group_load("x", "x", x_in, "out_L0")
        group_load("ctx", "ctx", ctx_in, "O_L3")
        group_load("side", "side", side_in, "norm_keys")

        blocks_transposed("T_ctx", "t_ctx", GROUP, ctx_in, lambda g: loaded("ctx", ctx_in, g), ctxT, "S_L3")
        layernorm("keys", [ctx_in, side_in], lambda g: [loaded("ctx", ctx_in, g), loaded("side", side_in, g)],
                  keys, EPS_L1, ["O_L1"])
        blocks_transposed("T_keys", "t_keys", A["L1"] * GROUP, keys, lambda g: "norm_keys", keysT, "S_L1")

        @step("V2")
        def _(g):
            pe.wait("t_ctx", g)
            bank = held["V2", g] = banks.take("v2", g)
            pe.wait("w_L2")
            wide_bias("L2v", bank)
            accumulate("V2", g, bank, [(b, c, Wv2[:]) for b, c in enumerate(blocks(at(ctxT, g), GROUP))])

        @step("v2")
        def _(g):
            engine = engine_of("v2")
            engine.wait("V2", g)
            engine.wait("OUT_L2", g - len(V2))
            evacuate("v2", g, [(flat(at(V2, g)), held.pop(("V2", g))[:], None)])

        @step("B2")
        def _(g):
            pe.wait("t_ctx", g)
            bank = held["B2", g] = banks.take("b2", g)
            pe.wait("M2T")
            for e in range(T):
                pe.op(mm, bank[:, e * TOK:(e + 1) * TOK], M2T[:, e * P:(e + 1) * P], at(ctxT, g)[:], start=True, stop=True,
                      done=("B2", g) if e == T - 1 else None)

        @step("b2")
        def _(g):
            engine = engine_of("b2")
            engine.wait("B2", g)
            engine.wait("k_bias2")
            engine.wait("S_L2", g - len(B2))
            bank = held.pop(("B2", g))
            evacuate("b2", g, [(at(B2, g)[:, e, :], bank[:, e * TOK:(e + 1) * TOK], k_bias2[:, e:e + 1]) for e in range(T)])

        transposed("L0", x_in, lambda g: loaded("x", x_in, g), "Q_L0")
        queries_and_scores("L0", ctxT, "t_ctx")
        softmax("L0", "PT_L0")
        attended("L0", ctx_in)
        project("L0")
        residual("L0", x_in, lambda g: loaded("x", x_in, g), x1, lambda g: ["norm_ln1", "out_L1"])

        layernorm("ln1", [x1], lambda g: ["out_L0"], xhat["ln1"], EPS_L1, ["T_L1"])
        transposed("L1", xhat["ln1"], lambda g: "norm_ln1", "Q_L1")
        queries_and_scores("L1", keysT, "t_keys")
        softmax("L1", "PT_L1")
        attended("L1", keys)
        project("L1")
        residual("L1", x1, lambda g: "out_L0", x2, lambda g: ["norm_lnf", "out_fc"])
        layernorm("lnf", [x2], lambda g: ["out_L1"], xhat["lnf"], EPS_L1, ["T_fc"])
        transposed("fc", xhat["lnf"], lambda g: "norm_lnf", "OUT_fc")

        @step("OUT_fc")
        def _(g):
            bank = held["OUT_fc", g] = banks.take("out_fc", g)
            wide_bias("fc", bank)
            pe.wait("F_lo")
            pe.wait("lo_fc", g)
            hi, lo = at(xT_hi["fc"], g), at(xT_lo["fc"], g)
            products = []
            for b in range(GROUP):
                for t in range(T):
                    s = slice(b * P, (b + 1) * P)
                    products += [(b, hi[:, t, s], F_hi[:, t, :]), (b, hi[:, t, s], F_lo[:, t, :]),
                                 (b, lo[:, t, s], F_hi[:, t, :])]
            accumulate("OUT_fc", g, bank, products)

        residual("fc", x2, lambda g: "out_L1", x3, lambda g: ["T_L2", "out_L2"])

        transposed("L2", x3, lambda g: "out_fc", "S_L2")

        @step("S_L2")
        def _(g):
            pe.wait("hi_L2", g)
            pe.wait("b2", g)
            bank = held["S_L2", g] = banks.take("exp_L2", g)
            for b in range(GROUP):
                s = slice(b * P, (b + 1) * P)
                for e in range(T):
                    pe.op(mm, bank[:, s], at(B2, g)[:, e, s], at(xT_hi["L2"], g)[:, e, s], start=e == 0, stop=e == T - 1,
                          done=("S_L2", g) if b == GROUP - 1 and e == T - 1 else None)

        softmax("L2", "OUT_L2")

        @step("OUT_L2")
        def _(g):
            pe.wait("prob_L2", g)
            pe.wait("v2", g)
            bank = held["OUT_L2", g] = banks.take("out_L2", g)
            for b in range(GROUP):
                pe.op(mm, bank[:, b * D:(b + 1) * D], at(prob["L2"], g)[:, b, :], at(V2, g)[:, b, :],
                      start=True, stop=True, done=("OUT_L2", g) if b == GROUP - 1 else None)

        residual("L2", x3, lambda g: "out_fc", x4, lambda g: ["norm_ln2"])
        layernorm("ln2", [x4], lambda g: ["out_L2"], xhat["ln2"], EPS_L2, ["T_L3", "x_res"])

        @step("x_res")
        def _(g):
            pool.wait("norm_ln2", g)
            pool.wait("gamma_row")
            pool.wait("out_L3", g - len(x_res))
            pool.op(nc.gpsimd.tensor_tensor, at(x_res, g)[:], at(xhat["ln2"], g)[:],
                    gamma_row[:].unsqueeze(1).to_broadcast([P, GROUP, D]), ALU.mult, done=("x_res", g))

        transposed("L3", xhat["ln2"], lambda g: "norm_ln2", "Q_L3")
        queries_and_scores("L3", ctxT, "t_ctx")
        softmax("L3", "PT_L3")
        attended("L3", ctx_in)
        project("L3")
        residual("L3", x_res, lambda g: "x_res", y, lambda g: [loaded("stored", y, g)])

        @step("store")
        def _(g):
            sp.wait("out_L3", g)
            sp.dma(nc.sync.dma_start, seqs(out, g), at(y, g)[:], done=(loaded("stored", y, g), g))

        order = [(STARTS[name] + g * PERIOD, g, name) for name in steps for g in range(GROUPS)]
        order += [(PREPARATIONS[name], -1, name) for name in preparations]
        for _, g, name in sorted(order):
            if g < 0:
                preparations[name]()
            else:
                steps[name](g)
        for g in range(GROUPS - len(y), GROUPS):
            sp.wait(loaded("stored", y, g), g)

        block = stack.enter_context(nc.Block())
        block.tensor(pe.play)
        block.scalar(act.play)
        block.vector(dve.play)
        block.gpsimd(pool.play)
        block.sync(sp.play)


def layout(inputs):
    import numpy as np

    def name(a, what):
        layer, side = a[:2], a[2:]
        return f"{layer}_xattn_{side + '_' if side else ''}{what}"

    arrays = {"x": inputs["x"], "ctx": inputs["ctx_512"], "side": inputs["fside_BxSxS_0"]}
    for a in ATTENTIONS + ["L2"]:
        arrays[f"{a}_WqT"] = inputs[name(a, "Wq")].T
        arrays[f"{a}_WkT"] = inputs[name(a, "Wk")].T
        if a != "L2":
            arrays[f"{a}_WvT"] = inputs[name(a, "Wv")].T
            arrays[f"{a}_Wo"] = inputs[name(a, "Wo")]
    arrays["L2_Wv"] = inputs["L2_xattn_Wv"]
    arrays["fc_W"] = inputs["L1_xattn_fc_W"]
    vectors = {"fc_g": "L1_xattn_ln_g", "fc_b": "L1_xattn_ln_b", "fc_bias": "L1_xattn_fc_b", "L2_bk": "L2_xattn_bk",
               "L2_bv": "L2_xattn_bv", "L3_g1": "L2_xattn_gamma", "L3_b1": "L2_xattn_beta"}
    for a in ATTENTIONS:
        for b in ("bq", "bv", "bo"):
            vectors[f"{a}_{b}"] = name(a, b)
    for a in ("L1a", "L1v"):
        for n in (1, 2):
            vectors[f"{a}_g{n}"] = name(a, f"ln{n}_g")
            vectors[f"{a}_b{n}"] = name(a, f"ln{n}_b")

    def padded(n):
        vector = inputs[vectors[n]]
        return np.concatenate([vector, np.zeros(D - vector.shape[0], vector.dtype)])

    arrays["cols"] = np.stack([padded(n).reshape(T, P) for n in COLS]).transpose(2, 0, 1).reshape(P, len(COLS) * T)
    arrays["rows"] = np.stack([padded(n) for n in ROWS])
    return {n: np.ascontiguousarray(a) for n, a in arrays.items()}


def kernel(**inputs):
    import numpy as np
    import concourse.bacc as bacc
    from concourse.bass_utils import run_bass_kernel_spmd

    nc = bacc.Bacc("TRN2", target_bir_lowering=False, num_devices=1)
    arrays = layout({n: np.asarray(a) for n, a in inputs.items()})
    ins = {n: nc.dram_tensor(f"in_{n}", a.shape, mybir.dt.from_np(a.dtype), kind="ExternalInput").ap()
           for n, a in arrays.items()}
    out = nc.dram_tensor("out", (BATCH, P, D), F32, kind="ExternalOutput").ap()
    build(nc, ins, out)
    result = run_bass_kernel_spmd(nc, [{f"in_{n}": a for n, a in arrays.items()}], core_ids=[0])
    return result.results[0]["out"]
```

```python
from contextlib import ExitStack

import concourse.bass as bass
from concourse import mybir

F32 = mybir.dt.float32
F32R = mybir.dt.float32r
ALU = mybir.AluOpType
ACT = mybir.ActivationFunctionType
AX = mybir.AxisListType

P = 128
D = 256
T = D // P
BATCH = 64
GROUP = 2
GROUPS = BATCH // GROUP
TOK = GROUP * P
BANKS = 8

STARTS = {"load_x": 0, "hi_L0": 107, "lo_L0": 281, "load_ctx": 580, "Q_L0": 626, "hi_ctx": 640, "q_L0": 727,
          "S_L0": 916, "lo_ctx": 928, "load_side": 1012, "max_L0": 1031, "exp_L0": 1074, "x_bias": 1279,
          "stats_keys": 1315, "rstd_keys": 1383, "PT_L0": 1417, "pT_L0": 1422, "B2": 1447, "inv_L0": 1658,
          "O_L0": 1732, "oT_hi_L0": 1806, "shift_keys": 1884, "oT_lo_L0": 1929, "norm_keys": 2113, "OUT_L0": 2190,
          "b2": 2219, "out_L0": 2285, "stats_ln1": 2349, "rstd_ln1": 2427, "shift_ln1": 2586, "T_keys": 2694,
          "norm_ln1": 2771, "T_L1": 3064, "t_keys": 3067, "hi_L1": 3142, "lo_L1": 3340, "Q_L1": 3473, "q_L1": 3541,
          "S_L1": 3839, "x1_bias": 3866, "max_L1": 4062, "exp_L1": 4196, "inv_L1": 4463, "prob_L1": 4536,
          "PT_L1": 4721, "pT_L1": 4781, "O_L1": 4964, "oT_hi_L1": 5075, "oT_lo_L1": 5282, "OUT_L1": 5629,
          "out_L1": 5740, "T_fc": 5955, "x2_bias": 6092, "hi_fc": 6142, "stats_lnf": 6169, "rstd_lnf": 6174,
          "lo_fc": 6272, "OUT_fc": 6508, "out_fc": 6585, "T_L2": 6768, "hi_L2": 6840, "S_L2": 7030, "max_L2": 7119,
          "exp_L2": 7170, "inv_L2": 7293, "prob_L2": 7302, "O_L2": 7490, "sums_L2": 7513, "oT_hi_L2": 7608,
          "oT_lo_L2": 7731, "x3_bias": 7827, "OUT_L2": 7854, "out_L2": 7930, "stats_ln2": 8106, "rstd_ln2": 8288,
          "shift_ln2": 8293, "norm_ln2": 8456, "T_L3": 8764, "hi_L3": 8880, "lo_L3": 8969, "Q_L3": 9246,
          "q_L3": 9290, "S_L3": 9479, "max_L3": 9586, "exp_L3": 9691, "x_res": 9695, "PT_L3": 9807, "pT_L3": 10143,
          "inv_L3": 10427, "O_L3": 10563, "oT_hi_L3": 10619, "oT_lo_L3": 10804, "OUT_L3": 11192, "out_L3": 11399,
          "store": 11871}
COMES = [0, 810, 1589, 3179, 4746, 6323, 7901, 9478, 11056, 12634, 14212, 15790, 17368, 18945, 20523, 22101, 23679,
         25257, 26834, 28412, 29990, 31568, 33146, 34724, 36301, 37879, 39457, 40223, 40999, 42614, 43393, 44175]
PREPARATIONS = {"load_first": -50, "constants": -40, "keys_L0": 81, "products_L0": 284, "vectors_L0": 406,
                "load_rest": 506, "keys_L1": 516, "products_L1": 626, "fc": 666, "L2": 968, "vectors_L1": 1238,
                "keys_L3": 2794, "products_L3": 2979, "vectors_L3": 3293}
COPIES = {"x_in": 3, "x_bias": 3, "x2_bias": 2, "token_sums": 2, "x3_bias": 2, "ctx_in": 10, "side_in": 3,
          "keys": 3, "keysT": 2, "B2": 6, "x1": 3, "x2": 2, "xhat_ln1": 2, "xhat_ln2": 2, "x3": 2, "x4": 2,
          "x_res": 3, "y": 2, "xT_hi_L0": 1, "xT_lo_L0": 1, "prob_L0": 1, "neg_max_L0": 2, "total_L0": 2,
          "inv_total_L0": 2, "qT_L0": 1, "probT_L0": 1, "oT_hi_L0": 1, "oT_lo_L0": 1, "xT_hi_L1": 1, "xT_lo_L1": 1,
          "prob_L1": 1, "neg_max_L1": 2, "total_L1": 2, "inv_total_L1": 2, "qT_L1": 1, "probT_L1": 1,
          "oT_hi_L1": 1, "oT_lo_L1": 1, "xT_hi_fc": 1, "xT_lo_fc": 1, "xT_hi_L2": 1, "prob_L2": 1, "neg_max_L2": 2,
          "total_L2": 2, "inv_total_L2": 2, "oT_hi_L2": 1, "oT_lo_L2": 1, "xT_hi_L3": 1, "xT_lo_L3": 1,
          "prob_L3": 1, "neg_max_L3": 2, "total_L3": 2, "inv_total_L3": 3, "qT_L3": 1, "probT_L3": 1,
          "oT_hi_L3": 1, "oT_lo_L3": 1, "stats_keys": 2, "mean_var_keys": 2, "var_eps_keys": 2, "rstd_keys": 2,
          "shift_keys": 2, "stats_ln1": 2, "mean_var_ln1": 2, "var_eps_ln1": 2, "rstd_ln1": 2, "shift_ln1": 2,
          "stats_lnf": 2, "mean_var_lnf": 2, "var_eps_lnf": 2, "rstd_lnf": 2, "stats_ln2": 2, "mean_var_ln2": 2,
          "var_eps_ln2": 2, "rstd_ln2": 2, "shift_ln2": 2, "ctxT_hi": 2, "ctxT_lo": 1, "x1_bias": 3}
ON_VECTOR = ()
ON_SCALAR = ('prob_L1',)

SCALE = float(D) ** -0.5
EPS_L1 = 1e-5
EPS_L2 = 1e-6

LAYERS = {"L0": ["L0"], "L1": ["L1a", "L1v"], "L3": ["L3"]}
ATTENTIONS = ["L0", "L1a", "L1v", "L3"]
COLS = ["L0_bq", "L0_bv", "L1a_bq", "L1a_bv", "L1a_g1", "L1a_b1", "L1v_bq", "L1v_bv", "L1v_g1", "L1v_b1",
        "L3_bq", "L3_bv", "L3_g1", "L3_b1", "L2_bk", "fc_g", "fc_b", "L1a_b2", "L1v_b2", "L1a_g2", "L1v_g2"]
ROWS = ["L0_bo", "L1a_bo", "L1v_bo", "L3_bo", "fc_bias", "L2_bv", "L3_b1", "L3_g1", "L1a_g2", "L1v_g2"]


class Marks:

    def __init__(self, nc, stack):
        self.nc, self.stack, self.sems, self.count, self.value, self.order = nc, stack, {}, {}, {}, {}

    NEVER = 1 << 30

    def raised(self, counter, step, group, increment):
        if counter not in self.sems:
            self.sems[counter] = self.stack.enter_context(self.nc.semaphore("s_" + counter))
            self.count[counter] = 0
        self.count[counter] += increment
        self.value[step, group] = counter, self.count[counter]
        self.order[step, group] = len(self.order)
        return self.sems[counter]

    def also(self, name, mark):
        self.value[name], self.order[name] = self.value[mark], self.order[mark]


class Queue:

    def __init__(self, marks, name):
        self.marks, self.name, self.items, self.reached = marks, name, [], {}

    def wait(self, step, group=0):
        if isinstance(group, int) and group < 0:
            return
        counter, value = self.marks.value[step, group]
        if self.reached.get(counter, 0) < value:
            self.reached[counter] = value
            sem = self.marks.sems[counter]
            self.items.append(lambda e: e.wait_ge(sem, value))

    def op(self, method, *args, done=None, **kw):
        if done is None:
            self.items.append(lambda e: method(*args, **kw))
        else:
            sem = self.marks.raised(self.name, *done, 1)
            self.items.append(lambda e: method(*args, **kw).then_inc(sem, 1))

    def dma(self, method, dst, src, done):
        sem = self.marks.raised(done[0], *done, 16)
        self.items.append(lambda e: method(dst, src).then_inc(sem, 16))

    def play(self, e):
        for item in self.items:
            item(e)


class Banks:

    def __init__(self, banks, pe, marks):
        self.banks, self.pe, self.marks = banks, pe, marks
        self.readers = [None] * len(banks)

    def take(self, step, group=0):
        order = [-1 if r is None else self.marks.order.get(r, self.marks.NEVER) for r in self.readers]
        n = order.index(min(order))
        assert order[n] < self.marks.NEVER, f"no bank for {step} {group}"
        if self.readers[n]:
            self.pe.wait(*self.readers[n])
        self.readers[n] = step, group
        return self.banks[n]


def build(nc, ins, out):
    stack = ExitStack()
    with stack:
        marks = Marks(nc, stack)
        pe, act, dve, pool, sp = (Queue(marks, n) for n in ("pe", "act", "dve", "pool", "sp"))
        mm, tr = nc.tensor.matmul, nc.tensor.transpose

        def sb(name, shape, dtype=F32, where=stack):
            return where.enter_context(nc.sbuf_tensor(name, shape, dtype))

        def ring(name, copies, shape, dtype=F32):
            return [sb(f"{name}_{i}", shape, dtype) for i in range(copies)]

        banks = Banks([stack.enter_context(nc.psum_tensor(f"bank{i}", [P, 512], F32)) for i in range(BANKS)], pe, marks)

        ident = sb("ident", [P, P])
        minus_half = sb("minus_half", [P, 2 * GROUP])
        ones_row = sb("ones_row", [1, P])
        ones_col = sb("ones_col", [P, 1])
        mean_of_D = sb("mean_of_D", [P, P])
        cols = sb("cols", [P, len(COLS), T])
        scaled_cols = sb("scaled_cols", [P, len(COLS), T])
        gamma_row = sb("gamma_row", [P, D])
        bias = {k: sb(f"bias_{k}", [P, D]) for k in ("L0", "L1", "fc", "L2v", "L3")}
        M_hi = {a: sb(f"M_hi_{a}", [P, T, P], F32R) for a in ATTENTIONS}
        M_lo = {a: sb(f"M_lo_{a}", [P, T, P], F32R) for a in ATTENTIONS}
        N_hi = {a: sb(f"N_hi_{a}", [P, D], F32R) for a in ATTENTIONS}
        N_lo = {a: sb(f"N_lo_{a}", [P, D], F32R) for a in ATTENTIONS}
        m_col = {a: sb(f"m_{a}", [P, 1]) for a in ATTENTIONS}
        F_hi, F_lo = sb("F_hi", [P, T, D], F32R), sb("F_lo", [P, T, D], F32R)
        M2T_hi, M2T_lo, k_bias2 = sb("M2T_hi", [P, D], F32R), sb("M2T_lo", [P, D], F32R), sb("k_bias2", [P, T])
        Wv2_hi, Wv2_lo = sb("Wv2_hi", [P, D], F32R), sb("Wv2_lo", [P, D], F32R)

        def ring(name, shape, dtype=F32):
            return [sb(f"{name}_{i}", shape, dtype) for i in range(COPIES[name])]

        A = {k: len(LAYERS.get(k, [k])) for k in ("L0", "L1", "L2", "L3")}
        x_in = ring("x_in", [P, 2, GROUP * D])
        ctx_in = ring("ctx_in", [P, 2 * GROUP, P])
        side_in = ring("side_in", [P, GROUP, P])
        keys = ring("keys", [P, A["L1"] * GROUP, P])
        keysT = ring("keysT", [P, A["L1"] * TOK])
        B2 = ring("B2", [P, T, TOK])
        ctxT_hi = ring("ctxT_hi", [P, TOK], F32R)
        ctxT_lo = ring("ctxT_lo", [P, TOK], F32R)
        x1 = ring("x1", [P, GROUP, D])
        x2 = ring("x2", [P, GROUP, D])
        x_bias = ring("x_bias", [P, GROUP, D])
        x1_bias = ring("x1_bias", [P, GROUP, D])
        x2_bias = ring("x2_bias", [P, GROUP, D])
        xhat = {"ln1": ring("xhat_ln1", [P, GROUP, D])}
        xT_hi, xT_lo, qT, prob, probT, oT_hi, oT_lo = ({} for _ in range(7))

        def layer_buffers(k):
            xT_hi[k] = ring(f"xT_hi_{k}", [P, T, TOK], F32 if k == "L2" else F32R)
            if k != "L2":
                xT_lo[k] = ring(f"xT_lo_{k}", [P, T, TOK], F32R)
            if k != "fc":
                prob[k] = ring(f"prob_{k}", [P, A[k] * GROUP, P])
            if k in LAYERS:
                qT[k] = ring(f"qT_{k}", [P, A[k] * TOK])
                probT[k] = ring(f"probT_{k}", [P, A[k] * TOK])
            if k != "fc":
                oT_hi[k] = ring(f"oT_hi_{k}", [P, A[k] * TOK], F32R)
                oT_lo[k] = ring(f"oT_lo_{k}", [P, A[k] * TOK], F32R)

        for k in ("L0", "L1", "fc"):
            layer_buffers(k)
        stats, mean_var, var_eps, rstd, shift = ({} for _ in range(5))
        for k, n in {"keys": A["L1"] * GROUP, "ln1": GROUP, "lnf": GROUP, "ln2": GROUP}.items():
            stats[k] = ring(f"stats_{k}", [P, n, 6])
            mean_var[k] = ring(f"mean_var_{k}", [P, n, 2])
            var_eps[k] = ring(f"var_eps_{k}", [P, n])
            rstd[k] = ring(f"rstd_{k}", [P, n])
            if k != "lnf":
                shift[k] = ring(f"shift_{k}", [P, n])
        neg_max, total, inv_total = {}, {}, {}
        for k in A:
            neg_max[k] = ring(f"neg_max_{k}", [P, A[k] * GROUP])
            total[k] = ring(f"total_{k}", [P, A[k] * GROUP])
            inv_total[k] = ring(f"inv_total_{k}", [P, A[k] * GROUP])

        stage, temp = {}, {}
        with ExitStack() as staging:
            for a in ATTENTIONS + ["L2"]:
                stage[a] = {"WqT": sb(f"WqT_{a}", [P, T, D], where=staging), "WkT": sb(f"WkT_{a}", [P, T, P], where=staging)}
                if a != "L2":
                    stage[a]["WvT"] = sb(f"WvT_{a}", [P, T, P], where=staging)
                    stage[a]["Wo"] = sb(f"Wo_{a}", [P, T, D], where=staging)
            fcW, fc_gained, fc_centred = (sb(n, [P, T, D], where=staging) for n in ("fcW", "fc_gained", "fc_centred"))
            Wv2 = sb("Wv2", [P, D], where=staging)
            rows = sb("rows", [1, len(ROWS), D], where=staging)
            for a in ATTENTIONS + ["fc"]:
                temp[a] = {"bv": sb(f"rep_bv_{a}", [P, T, P], where=staging)}
            for a in ("L1a", "L1v"):
                temp[a]["N0"] = sb(f"N0_{a}", [P, D], where=staging)
                temp[a]["b2"] = sb(f"rep_b2_{a}", [P, P], where=staging)
            for a in ("L1a", "L1v", "L3"):
                temp[a]["M0"] = sb(f"M0_{a}", [P, T, P], where=staging)
        x3 = ring("x3", [P, GROUP, D])
        token_sums = ring("token_sums", [P, GROUP])
        x3_bias = ring("x3_bias", [P, GROUP, D])
        x4 = ring("x4", [P, GROUP, D])
        xhat["ln2"] = ring("xhat_ln2", [P, GROUP, D])
        layer_buffers("L2")
        layer_buffers("L3")
        x_res = ring("x_res", [P, GROUP, D])
        y = ring("y", [P, GROUP, D])

        def at(buffers, g):
            return buffers[g % len(buffers)]

        v = nc.vector
        LN = ("L1a", "L1v", "L3")
        LN_KEYS = ("L1a", "L1v")

        def col(name, t=0, of=cols):
            n = COLS.index(name)
            return of[:, n, t:t + 1]

        def row(name, width=D):
            return rows[0:1, ROWS.index(name), 0:width]

        def load(dst, src, stream):
            sp.dma(nc.sync.dma_start, dst, src, done=(stream, 0))

        def load_weights(a):
            for w in stage[a]:
                load(stage[a][w][:], ins[f"{a}_{w}"].rearrange("(t p) n -> p t n", p=P), f"w_{a}")

        def load_first():
            load(cols[:], ins["cols"].rearrange("p (n t) -> p n t", t=T), "vectors")
            load(rows[:], ins["rows"].rearrange("(o n) d -> o n d", o=1), "vectors")
            load_weights("L0")

        def load_rest():
            load_weights("L1a")
            load_weights("L1v")
            load_weights("L2")
            load(Wv2[:], ins["L2_Wv"], "w_L2")
            load(fcW[:], ins["fc_W"].rearrange("(t p) n -> p t n", p=P), "w_fc")
            load_weights("L3")

        def constants():
            pool.op(nc.gpsimd.memset, ident[:], 0.0, done=("zeroed", 0))
            pool.wait("zeroed")
            pool.op(nc.gpsimd.affine_select, out=ident[:], in_=ident[:], compare_op=ALU.not_equal, fill=1.0,
                    base=0, pattern=[[-1, P]], channel_multiplier=1, done=("ident", 0))
            pool.op(nc.gpsimd.memset, minus_half[:], -0.5)
            pool.op(nc.gpsimd.memset, ones_row[:], 1.0)
            pool.op(nc.gpsimd.memset, ones_col[:], 1.0)
            pool.op(nc.gpsimd.memset, mean_of_D[:], 1.0 / D, done=("constants", 0))
            pe.wait("constants")
            dve.wait("constants")
            act.wait("constants")
            dve.wait("vectors")
            dve.op(v.tensor_scalar, scaled_cols[:].rearrange("p n t -> p (n t)"), cols[:].rearrange("p n t -> p (n t)"),
                   SCALE, None, ALU.mult, done=("scaled", 0))
            for q in (pe, act, pool):
                q.wait("vectors")
            pe.wait("scaled")
            act.wait("scaled")
            dve.wait("scaled")

        def replicate(a, name, what, n):
            for t in range(n):
                pool.op(nc.gpsimd.tensor_copy, temp[a][what][:, t, :] if n > 1 else temp[a][what][:],
                        col(name, t).to_broadcast([P, P]), done=(f"rep_{what}", a))

        def bias_row(key, bank, produced):
            act.wait(*produced)
            act.op(nc.scalar.activation, bias[key][:], bank[:, 0:D], ACT.Copy, done=("bias", key))

        def split_product(hi, lo, bank, produced, name, a, scales):
            width = D // len(scales)
            act.wait(*produced)
            dve.wait(*produced)
            for i, scale in enumerate(scales):
                s = slice(i * width, (i + 1) * width)
                act.op(nc.scalar.activation, hi[:, s], bank[:, s], ACT.Copy, scale=scale, done=(f"{name}_hi", a))
            dve.wait(f"{name}_hi", a)
            for i, scale in enumerate(scales):
                s = slice(i * width, (i + 1) * width)
                dve.op(v.scalar_tensor_tensor, out=lo[:, s], in0=bank[:, s], scalar=scale, in1=hi[:, s].bitcast(F32),
                       op0=ALU.mult, op1=ALU.subtract, done=(f"{name}_lo", a))

        def prep_keys(a):
            w = stage[a]
            replicate(a, f"{a}_bv", "bv", T)
            if a in LN_KEYS:
                replicate(a, f"{a}_b2", "b2", 1)
                bank = banks.take("WkT", a)
                pe.op(mm, bank[:, 0:P], ones_row[:], row(f"{a}_g2", P), start=True, stop=True, done=("gain", a))
                dve.wait("gain", a)
                dve.wait(f"w_{a}")
                for t in range(T):
                    dve.op(v.tensor_tensor, w["WkT"][:, t, :], w["WkT"][:, t, :], bank[:, 0:P], ALU.mult, done=("WkT", a))

        def prep_products(a):
            w = stage[a]
            pe.wait(f"w_{a}")
            if a in LN_KEYS:
                pe.wait("WkT", a)
            bank_M, bank_N = banks.take("M_done", a), None
            for e in range(T):
                for h in range(T):
                    pe.op(mm, bank_M[:, e * P:(e + 1) * P], w["WqT"][:, h, e * P:(e + 1) * P], w["WkT"][:, h, :],
                          start=h == 0, stop=h == T - 1, done=("prod_M", a))
            bank_N = banks.take("N_done", a)
            for h in range(T):
                pe.op(mm, bank_N[:, 0:D], w["WvT"][:, h, :], w["Wo"][:, h, :], start=h == 0, stop=h == T - 1,
                      done=("prod_N", a))
            gains = [col(f"{a}_g1", t, scaled_cols) for t in range(T)] if a in LN else [SCALE]
            M_flat = [x[a][:].rearrange("p t d -> p (t d)") for x in (M_hi, M_lo)]
            act.wait("prod_M", a)
            if a in LN:
                act.op(nc.scalar.activation, temp[a]["M0"][:].rearrange("p t d -> p (t d)"), bank_M[:, 0:D], ACT.Copy,
                       done=("M0", a))
            split_product(*M_flat, bank_M, ("prod_M", a), "M", a, gains)
            marks.also(("M_done", a), ("M_lo", a))
            act.wait("prod_N", a)
            if a in LN_KEYS:
                act.op(nc.scalar.activation, temp[a]["N0"][:], bank_N[:, 0:D], ACT.Copy, done=("N0", a))
            split_product(N_hi[a], N_lo[a], bank_N, ("prod_N", a), "N", a, [col(f"{a}_g2")] if a in LN_KEYS else [1.0])
            marks.also(("N_done", a), ("N_lo", a))

        def prep_m(a):
            w = stage[a]
            bank = banks.take("m", a)
            terms = [(w["WkT"][:, h, :], col(f"{a}_bq", h, scaled_cols)) for h in range(T)]
            if a in LN:
                pe.wait("M0", a)
                terms += [(temp[a]["M0"][:, e, :], col(f"{a}_b1", e, scaled_cols)) for e in range(T)]
            for n, (stationary, moving) in enumerate(terms):
                pe.op(mm, bank[:, 0:1], stationary, moving, start=n == 0, stop=n == len(terms) - 1, done=("prod_m", a))
            act.wait("prod_m", a)
            act.op(nc.scalar.activation, m_col[a][:], bank[:, 0:1], ACT.Copy, done=("m", a))

        def prep_bias(key, attentions, extra):
            bank = banks.take("bias", key)
            terms = []
            for a in attentions:
                pe.wait("rep_bv", a)
                terms += [(temp[a]["bv"][:, h, :], stage[a]["Wo"][:, h, :]) for h in range(T)]
                if a in LN_KEYS:
                    pe.wait("rep_b2", a)
                    pe.wait("N0", a)
                    terms += [(temp[a]["b2"][:], temp[a]["N0"][:])]
            terms += [(ones_row[:], row(r)) for r in extra]
            for n, (stationary, moving) in enumerate(terms):
                pe.op(mm, bank[:, 0:D], stationary, moving, start=n == 0, stop=n == len(terms) - 1, done=("prod_n", key))
            bias_row(key, bank, ("prod_n", key))

        def prep_fc():
            replicate("fc", "fc_b", "bv", T)
            act.wait("w_fc")
            for t in range(T):
                act.op(nc.scalar.activation, fc_gained[:, t, :], fcW[:, t, :], ACT.Copy, scale=col("fc_g", t), done=("fc_gained", 0))
            pe.wait("w_fc")
            pe.wait("rep_bv", "fc")
            bank = banks.take("bias", "fc")
            terms = [(temp["fc"]["bv"][:, t, :], fcW[:, t, :]) for t in range(T)] + [(ones_row[:], row("fc_bias"))]
            for n, (stationary, moving) in enumerate(terms):
                pe.op(mm, bank[:, 0:D], stationary, moving, start=n == 0, stop=n == len(terms) - 1, done=("prod_n", "fc"))
            bias_row("fc", bank, ("prod_n", "fc"))
            pe.wait("fc_gained")
            bank = banks.take("fc_centred")
            for t in range(T):
                pe.op(mm, bank[:, 0:D], mean_of_D[:], fc_gained[:, t, :], start=t == 0, stop=t == T - 1, done=("fc_mean", 0))
            dve.wait("fc_mean")
            for t in range(T):
                dve.op(v.tensor_tensor, fc_centred[:, t, :], fc_gained[:, t, :], bank[:, 0:D], ALU.subtract,
                       done=("fc_centred", 0))
            act.wait("fc_centred")
            act.op(nc.scalar.activation, F_hi[:], fc_centred[:], ACT.Copy, done=("F_hi", 0))
            dve.wait("F_hi")
            dve.op(v.tensor_tensor, F_lo[:], fc_centred[:], F_hi[:].bitcast(F32), ALU.subtract, done=("F_lo", 0))

        def prep_L2():
            w = stage["L2"]
            pe.wait("w_L2")
            bank = banks.take("M_lo", "L2")
            for h in range(T):
                pe.op(mm, bank[:, 0:D], w["WkT"][:, h, :], w["WqT"][:, h, :], start=h == 0, stop=h == T - 1,
                      done=("prod_M", "L2"))
            split_product(M2T_hi, M2T_lo, bank, ("prod_M", "L2"), "M", "L2", [SCALE])
            bank = banks.take("k_bias2")
            for e in range(T):
                for h in range(T):
                    pe.op(mm, bank[:, e:e + 1], w["WqT"][:, h, e * P:(e + 1) * P], col("L2_bk", h, scaled_cols),
                          start=h == 0, stop=h == T - 1, done=("prod_m", "L2"))
            act.wait("prod_m", "L2")
            act.op(nc.scalar.activation, k_bias2[:], bank[:, 0:T], ACT.Copy, done=("k_bias2", 0))
            bank = banks.take("bias", "L2v")
            pe.op(mm, bank[:, 0:D], ones_row[:], row("L2_bv"), start=True, stop=True, done=("prod_n", "L2"))
            bias_row("L2v", bank, ("prod_n", "L2"))
            act.wait("w_L2")
            act.op(nc.scalar.activation, Wv2_hi[:], Wv2[:], ACT.Copy, done=("Wv2_hi", 0))
            dve.wait("Wv2_hi")
            dve.op(v.tensor_tensor, Wv2_lo[:], Wv2[:], Wv2_hi[:].bitcast(F32), ALU.subtract, done=("N_lo", "L2"))

        def prep_gamma():
            bank = banks.take("gamma_row")
            pe.op(mm, bank[:, 0:D], ones_row[:], row("L3_g1"), start=True, stop=True, done=("spread", 0))
            act.wait("spread")
            act.op(nc.scalar.activation, gamma_row[:], bank[:, 0:D], ACT.Copy, done=("gamma_row", 0))

        preparations = {
            "load_first": load_first, "constants": constants, "load_rest": load_rest,
            "keys_L0": lambda: prep_keys("L0"), "products_L0": lambda: prep_products("L0"),
            "vectors_L0": lambda: (prep_m("L0"), prep_bias("L0", ["L0"], ["L0_bo"])),
            "keys_L1": lambda: (prep_keys("L1a"), prep_keys("L1v")),
            "products_L1": lambda: (prep_products("L1a"), prep_products("L1v")),
            "vectors_L1": lambda: (prep_m("L1a"), prep_m("L1v"), prep_bias("L1", ["L1a", "L1v"], ["L1a_bo", "L1v_bo"])),
            "L2": prep_L2, "fc": prep_fc,
            "keys_L3": lambda: prep_keys("L3"), "products_L3": lambda: prep_products("L3"),
            "vectors_L3": lambda: (prep_m("L3"), prep_bias("L3", ["L3"], ["L3_bo", "L3_b1"]), prep_gamma()),
        }

        steps = {}
        held = {}

        def step(name):
            def keep(function):
                steps[name] = function
                return function
            return keep

        def evacuate(name, g, pieces):
            for i, (dst, src, bias) in enumerate(pieces):
                done = (name, g) if i == len(pieces) - 1 else None
                if name in ON_VECTOR and bias is None:
                    dve.op(v.tensor_copy, dst, src, done=done)
                elif name in ON_VECTOR:
                    dve.op(v.tensor_scalar, dst, src, bias, None, ALU.add, done=done)
                elif bias is None:
                    act.op(nc.scalar.activation, dst, src, ACT.Copy, done=done)
                else:
                    act.op(nc.scalar.activation, dst, src, ACT.Identity, bias=bias, done=done)

        def engine_of(name, usual=act):
            return dve if name in ON_VECTOR else act if name in ON_SCALAR else usual

        def blocks(bank, n):
            return [bank[:, b * P:(b + 1) * P] for b in range(n)]

        def loaded(what, ring, g):
            return f"{what}{g % len(ring)}"

        def split_evacuation(produced, hi_step, lo_step, hi, lo, freed_by):
            @step(hi_step)
            def _(g):
                engine = engine_of(hi_step)
                engine.wait(produced, g)
                engine.wait(freed_by, g - len(hi))
                evacuate(hi_step, g, [(flat(at(hi, g)), flat_like(held[produced, g], hi), None)])

            @step(lo_step)
            def _(g):
                dve.wait(hi_step, g)
                dve.wait(freed_by, g - len(lo))
                dve.op(v.tensor_tensor, flat(at(lo, g)), flat_like(held.pop((produced, g)), hi),
                       flat(at(hi, g)).bitcast(F32), ALU.subtract, done=(lo_step, g))

        def flat(tile):
            return tile[:] if len(tile.shape) == 2 else tile[:].rearrange("p a n -> p (a n)")

        def flat_like(bank, ring):
            n = 1
            for extent in ring[0].shape[1:]:
                n *= extent
            return bank[:, 0:n]

        def transposed(k, src, after, freed_by):
            @step(f"T_{k}")
            def _(g):
                pe.wait(after(g), g)
                last = f"hi_{k}" if k == "L2" else f"lo_{k}"
                bank = held[f"T_{k}", g] = banks.take(last, g)
                for t in range(T):
                    for b in range(GROUP):
                        n = t * GROUP + b
                        pe.op(tr, bank[:, n * P:(n + 1) * P], at(src, g)[:, b, t * P:(t + 1) * P], ident[:],
                              done=(f"T_{k}", g) if n == T * GROUP - 1 else None)

            if k != "L2":
                split_evacuation(f"T_{k}", f"hi_{k}", f"lo_{k}", xT_hi[k], xT_lo[k], freed_by)
            else:
                @step(f"hi_{k}")
                def _(g):
                    engine = engine_of(f"hi_{k}")
                    engine.wait(f"T_{k}", g)
                    engine.wait(freed_by, g - len(xT_hi[k]))
                    evacuate(f"hi_{k}", g, [(flat(at(xT_hi[k], g)), held.pop((f"T_{k}", g))[:], None)])

        def blocks_transposed(produce, evacuated, n, src, after, dst, freed_by):
            @step(produce)
            def _(g):
                pe.wait(after(g), g)
                bank = held[produce, g] = banks.take(evacuated, g)
                for b, block in enumerate(blocks(bank, n)):
                    pe.op(tr, block, at(src, g)[:, b, :], ident[:], done=(produce, g) if b == n - 1 else None)

            @step(evacuated)
            def _(g):
                engine = engine_of(evacuated)
                engine.wait(produce, g)
                engine.wait(freed_by, g - len(dst))
                evacuate(evacuated, g, [(at(dst, g)[:], held.pop((produce, g))[:, 0:n * P], None)])

        def queries_and_scores(k, kT, after):
            @step(f"Q_{k}")
            def _(g):
                bank = held[f"Q_{k}", g] = banks.take(f"q_{k}", g)
                pe.wait(f"lo_{k}", g)
                for a in LAYERS[k]:
                    pe.wait("M_lo", a)
                hi, lo = at(xT_hi[k], g), at(xT_lo[k], g)
                for i, a in enumerate(LAYERS[k]):
                    passes = [(w, x, t) for t in range(T) for w, x in ((M_hi[a], hi), (M_lo[a], hi), (M_hi[a], lo))]
                    for n, (w, x, t) in enumerate(passes):
                        last = n == len(passes) - 1
                        pe.op(mm, bank[:, i * TOK:(i + 1) * TOK], w[:, t, :], x[:, t, :], start=n == 0, stop=last,
                              done=(f"Q_{k}", g) if last and i == A[k] - 1 else None)

            @step(f"q_{k}")
            def _(g):
                engine = engine_of(f"q_{k}")
                engine.wait(f"Q_{k}", g)
                engine.wait("m", LAYERS[k][-1])
                engine.wait(f"S_{k}", g - len(qT[k]))
                bank = held.pop((f"Q_{k}", g))
                evacuate(f"q_{k}", g, [(at(qT[k], g)[:, i * TOK:(i + 1) * TOK], bank[:, i * TOK:(i + 1) * TOK],
                                        m_col[a][:, 0:1]) for i, a in enumerate(LAYERS[k])])

            @step(f"S_{k}")
            def _(g):
                pe.wait(after(g), g)
                pe.wait(f"q_{k}", g)
                bank = held[f"S_{k}", g] = banks.take(f"exp_{k}", g)
                n = A[k] * GROUP
                for b, (block, q, c) in enumerate(zip(blocks(bank, n), blocks(at(qT[k], g), n), blocks(kT(g), n))):
                    pe.op(mm, block, q, c, start=True, stop=True, done=(f"S_{k}", g) if b == n - 1 else None)

        def softmax(k, freed_by, divided_by):
            n = A[k] * GROUP

            @step(f"max_{k}")
            def _(g):
                dve.wait(f"S_{k}", g)
                dve.wait(f"exp_{k}", g - len(neg_max[k]))
                dve.op(v.tensor_reduce, at(neg_max[k], g)[:], held[f"S_{k}", g][:, 0:n * P].rearrange("p (b k) -> p b k", k=P),
                       AX.X, ALU.max, negate=True, done=(f"max_{k}", g))

            @step(f"exp_{k}")
            def _(g):
                act.wait(f"max_{k}", g)
                act.wait(freed_by, g - len(prob[k]))
                act.wait(f"inv_{k}", g - len(total[k]))
                for b, block in enumerate(blocks(held.pop((f"S_{k}", g)), n)):
                    act.op(nc.scalar.activation, at(prob[k], g)[:, b, :], block, ACT.Exp,
                           bias=at(neg_max[k], g)[:, b:b + 1], accum_out=at(total[k], g)[:, b:b + 1],
                           done=(f"exp_{k}", g) if b == n - 1 else None)

            @step(f"inv_{k}")
            def _(g):
                dve.wait(f"exp_{k}", g)
                dve.wait(divided_by, g - len(inv_total[k]))
                dve.op(v.reciprocal, at(inv_total[k], g)[:], at(total[k], g)[:], done=(f"inv_{k}", g))

            if divided_by != f"prob_{k}":
                return

            @step(f"prob_{k}")
            def _(g):
                engine = engine_of(f"prob_{k}", pool)
                engine.wait(f"inv_{k}", g)
                p = at(prob[k], g)
                for b in range(n):
                    done = (f"prob_{k}", g) if b == n - 1 else None
                    scale = at(inv_total[k], g)[:, b:b + 1]
                    if engine is act:
                        act.op(nc.scalar.activation, p[:, b, :], p[:, b, :], ACT.Copy, scale=scale, done=done)
                    elif engine is dve:
                        dve.op(v.tensor_scalar, p[:, b, :], p[:, b, :], scale, None, ALU.mult, done=done)
                    else:
                        pool.op(nc.gpsimd.tensor_scalar, p[:, b, :], p[:, b, :], scale, 1.0, ALU.mult, ALU.mult, done=done)

        def attended(k, natural, after):
            blocks_transposed(f"PT_{k}", f"pT_{k}", A[k] * GROUP, prob[k], lambda g: after, probT[k], f"O_{k}")

            @step(f"O_{k}")
            def _(g):
                pe.wait(f"pT_{k}", g)
                bank = held[f"O_{k}", g] = banks.take(f"oT_lo_{k}", g)
                n = A[k] * GROUP
                for b, (block, p) in enumerate(zip(blocks(bank, n), blocks(at(probT[k], g), n))):
                    pe.op(mm, block, at(natural, g)[:, b, :], p, start=True, stop=True,
                          done=(f"O_{k}", g) if b == n - 1 else None)

            split_evacuation(f"O_{k}", f"oT_hi_{k}", f"oT_lo_{k}", oT_hi[k], oT_lo[k], f"OUT_{k}")

        def project(k, weights):
            @step(f"OUT_{k}")
            def _(g):
                bank = held[f"OUT_{k}", g] = banks.take(f"out_{k}", g)
                for a, _, _ in weights:
                    pe.wait("N_lo", a)
                pe.wait(f"oT_lo_{k}", g)
                hi, lo = at(oT_hi[k], g), at(oT_lo[k], g)
                products = []
                for b in range(GROUP):
                    for i, (_, N_h, N_l) in enumerate(weights):
                        s = slice((i * GROUP + b) * P, (i * GROUP + b + 1) * P)
                        products += [(b, hi[:, s], N_h[:]), (b, hi[:, s], N_l[:]), (b, lo[:, s], N_h[:])]
                accumulate(f"OUT_{k}", g, bank, products)

        def N_of(k):
            return [(a, N_hi[a], N_lo[a]) for a in LAYERS[k]]

        def accumulate(name, g, bank, products):
            for n, (b, stationary, moving) in enumerate(products):
                pe.op(mm, bank[:, b * D:(b + 1) * D], stationary, moving,
                      start=n == 0 or products[n - 1][0] != b, stop=n == len(products) - 1 or products[n + 1][0] != b,
                      done=(name, g) if n == len(products) - 1 else None)

        def residual(k, add, after, dst, freed_by, scale=None):
            @step(f"out_{k}")
            def _(g):
                dve.wait(f"OUT_{k}", g)
                for w in after:
                    dve.wait(w, g)
                for r in freed_by(g - len(dst)):
                    dve.wait(r, g - len(dst))
                bank = held.pop((f"OUT_{k}", g))
                if scale is None:
                    dve.op(v.tensor_tensor, flat(at(dst, g)), bank[:], flat(at(add, g)), ALU.add, done=(f"out_{k}", g))
                    return
                for b in range(GROUP):
                    dve.op(v.scalar_tensor_tensor, out=at(dst, g)[:, b, :], in0=bank[:, b * D:(b + 1) * D],
                           scalar=at(scale, g)[:, b:b + 1], in1=at(add, g)[:, b, :], op0=ALU.mult, op1=ALU.add,
                           done=(f"out_{k}", g) if b == GROUP - 1 else None)

        def plus_row(name, key, src, view, after, dst, freed_by):
            @step(name)
            def _(g):
                pool.wait("bias", key)
                pool.wait(after(g), g)
                pool.wait(freed_by, g - len(dst))
                pool.op(nc.gpsimd.tensor_tensor, at(dst, g)[:], view(at(src, g)),
                        bias[key][:].unsqueeze(1).to_broadcast([P, GROUP, D]), ALU.add, done=(name, g))

        def moments(k, sources, after, eps, mean_read_by, rstd_read_by):
            tiles = [(ring, b) for ring in sources for b in range(GROUP)]

            @step(f"stats_{k}")
            def _(g):
                st, mv = at(stats[k], g), at(mean_var[k], g)
                for w in after(g):
                    dve.wait(w, g)
                dve.wait(f"mv_{k}", g - len(stats[k]))
                for n, (src, b) in enumerate(tiles):
                    dve.op(v.bn_stats, st[:, n, :], at(src, g)[:, b, :], done=(f"st_{k}", g) if n == len(tiles) - 1 else None)
                dve.wait(f"st_{k}", g)
                dve.wait(mean_read_by, g - len(mean_var[k]))
                for n in range(len(tiles)):
                    dve.op(v.bn_aggr, mv[:, n, :], st[:, n, :], done=(f"mv_{k}", g) if n == len(tiles) - 1 else None)
                dve.wait(f"mv_{k}", g)
                dve.wait(f"rstd_{k}", g - len(var_eps[k]))
                dve.op(v.tensor_scalar, at(var_eps[k], g)[:], mv[:, :, 1], eps, None, ALU.add, done=(f"ve_{k}", g))

            @step(f"rstd_{k}")
            def _(g):
                pool.wait(f"ve_{k}", g)
                pool.wait("constants")
                pool.wait(rstd_read_by, g - len(rstd[k]))
                pool.op(nc.gpsimd.tensor_tensor, at(rstd[k], g)[:], at(var_eps[k], g)[:], minus_half[:, 0:len(tiles)],
                        ALU.pow, done=(f"rstd_{k}", g))

        def layernorm(k, sources, after, dst, freed_by):
            tiles = [(ring, b) for ring in sources for b in range(GROUP)]

            @step(f"shift_{k}")
            def _(g):
                dve.wait(f"rstd_{k}", g)
                dve.wait(f"norm_{k}", g - len(shift[k]))
                dve.op(v.scalar_tensor_tensor, out=at(shift[k], g)[:], in0=at(mean_var[k], g)[:, :, 0], scalar=-1.0,
                       in1=at(rstd[k], g)[:], op0=ALU.mult, op1=ALU.mult, done=(f"shift_{k}", g))

            @step(f"norm_{k}")
            def _(g):
                engine = engine_of(f"norm_{k}", pool)
                for w in after(g):
                    engine.wait(w, g)
                engine.wait(f"shift_{k}", g)
                for r in freed_by:
                    engine.wait(r, g - len(dst))
                for n, (src, b) in enumerate(tiles):
                    done = (f"norm_{k}", g) if n == len(tiles) - 1 else None
                    to, of = at(dst, g)[:, n, :], at(src, g)[:, b, :]
                    scale, offset = at(rstd[k], g)[:, n:n + 1], at(shift[k], g)[:, n:n + 1]
                    if engine is act:
                        act.op(nc.scalar.activation, to, of, ACT.Identity, bias=offset, scale=scale, done=done)
                    else:
                        method = v.tensor_scalar if engine is dve else nc.gpsimd.tensor_scalar
                        engine.op(method, to, of, scale, offset, ALU.mult, ALU.add, done=done)

        def seqs(tensor, g):
            return tensor[g * GROUP:(g + 1) * GROUP].rearrange("b p e -> p b e")

        def group_load(what, ring, freed_by):
            @step(f"load_{what}")
            def _(g):
                for r in freed_by:
                    sp.wait(r, g - len(ring))
                tile = at(ring, g)[:].rearrange("p a n -> p (a n)")
                sp.dma(nc.sync.dma_start, tile, ins[what][g], done=(loaded(what, ring, g), g))

        def x_loaded(g):
            return loaded("x", x_in, g)

        def ctx_loaded(g):
            return loaded("ctx", ctx_in, g)

        group_load("x", x_in, ["x_bias", "lo_L0"])
        group_load("ctx", ctx_in, ["O_L3"])
        group_load("side", side_in, ["norm_keys"])

        def ctxT(g):
            return at(ctx_in, g)[:, GROUP:2 * GROUP, :].rearrange("p b n -> p (b n)")

        moments("keys", [ctx_in, side_in], lambda g: [ctx_loaded(g), loaded("side", side_in, g)], EPS_L1,
                "shift_keys", "norm_keys")
        layernorm("keys", [ctx_in, side_in], lambda g: [ctx_loaded(g), loaded("side", side_in, g)], keys, ["O_L1"])
        blocks_transposed("T_keys", "t_keys", A["L1"] * GROUP, keys, lambda g: "norm_keys", keysT, "S_L1")

        @step("hi_ctx")
        def _(g):
            act.wait(ctx_loaded(g), g)
            act.wait("B2", g - len(ctxT_hi))
            act.op(nc.scalar.activation, at(ctxT_hi, g)[:], ctxT(g), ACT.Copy, done=("hi_ctx", g))

        @step("lo_ctx")
        def _(g):
            pool.wait(ctx_loaded(g), g)
            pool.wait("hi_ctx", g)
            pool.wait("B2", g - len(ctxT_lo))
            pool.op(nc.gpsimd.tensor_tensor, at(ctxT_lo, g)[:], ctxT(g), at(ctxT_hi, g)[:].bitcast(F32), ALU.subtract,
                    done=("lo_ctx", g))

        @step("B2")
        def _(g):
            pe.wait("lo_ctx", g)
            bank = held["B2", g] = banks.take("b2", g)
            pe.wait("M_lo", "L2")
            hi, lo = at(ctxT_hi, g), at(ctxT_lo, g)
            for e in range(T):
                s = slice(e * P, (e + 1) * P)
                passes = [(M2T_hi, hi), (M2T_lo, hi), (M2T_hi, lo)]
                for n, (w, c) in enumerate(passes):
                    pe.op(mm, bank[:, e * TOK:(e + 1) * TOK], w[:, s], c[:], start=n == 0, stop=n == len(passes) - 1,
                          done=("B2", g) if e == T - 1 and n == len(passes) - 1 else None)

        @step("b2")
        def _(g):
            engine = engine_of("b2")
            engine.wait("B2", g)
            engine.wait("k_bias2")
            engine.wait("S_L2", g - len(B2))
            bank = held.pop(("B2", g))
            evacuate("b2", g, [(at(B2, g)[:, e, :], bank[:, e * TOK:(e + 1) * TOK], k_bias2[:, e:e + 1]) for e in range(T)])

        plus_row("x_bias", "L0", x_in, lambda tile: tile[:, 0, :].rearrange("p (b d) -> p b d", d=D), x_loaded, x_bias, "out_L0")

        @step("hi_L0")
        def _(g):
            act.wait(x_loaded(g), g)
            act.wait("Q_L0", g - len(xT_hi["L0"]))
            act.op(nc.scalar.activation, flat(at(xT_hi["L0"], g)), at(x_in, g)[:, 1, :], ACT.Copy, done=("hi_L0", g))

        @step("lo_L0")
        def _(g):
            engine, method = (dve, v.tensor_tensor) if "lo_L0" in ON_VECTOR else (pool, nc.gpsimd.tensor_tensor)
            engine.wait(x_loaded(g), g)
            engine.wait("hi_L0", g)
            engine.wait("Q_L0", g - len(xT_lo["L0"]))
            engine.op(method, flat(at(xT_lo["L0"], g)), at(x_in, g)[:, 1, :], flat(at(xT_hi["L0"], g)).bitcast(F32),
                   ALU.subtract, done=("lo_L0", g))

        queries_and_scores("L0", ctxT, ctx_loaded)
        softmax("L0", "PT_L0", "out_L0")
        attended("L0", ctx_in, "exp_L0")
        project("L0", N_of("L0"))
        residual("L0", x_bias, ["x_bias", "inv_L0"], x1, lambda g: ["norm_ln1", "x1_bias"], inv_total["L0"])

        moments("ln1", [x1], lambda g: ["out_L0"], EPS_L1, "shift_ln1", "norm_ln1")
        layernorm("ln1", [x1], lambda g: ["out_L0"], xhat["ln1"], ["T_L1"])
        transposed("L1", xhat["ln1"], lambda g: "norm_ln1", "Q_L1")
        queries_and_scores("L1", lambda g: at(keysT, g), lambda g: "t_keys")
        softmax("L1", "PT_L1", "prob_L1")
        attended("L1", keys, "prob_L1")
        project("L1", N_of("L1"))
        plus_row("x1_bias", "L1", x1, lambda tile: tile[:], lambda g: "out_L0", x1_bias, "out_L1")
        residual("L1", x1_bias, ["x1_bias"], x2, lambda g: ["x2_bias", "T_fc"])

        moments("lnf", [x2], lambda g: ["out_L1"], EPS_L1, "ve_lnf", "out_fc")
        plus_row("x2_bias", "fc", x2, lambda tile: tile[:], lambda g: "out_L1", x2_bias, "out_fc")
        transposed("fc", x2, lambda g: "out_L1", "OUT_fc")

        @step("OUT_fc")
        def _(g):
            bank = held["OUT_fc", g] = banks.take("out_fc", g)
            pe.wait("F_lo")
            pe.wait("lo_fc", g)
            hi, lo = at(xT_hi["fc"], g), at(xT_lo["fc"], g)
            products = []
            for b in range(GROUP):
                for t in range(T):
                    s = slice(b * P, (b + 1) * P)
                    products += [(b, hi[:, t, s], F_hi[:, t, :]), (b, hi[:, t, s], F_lo[:, t, :]),
                                 (b, lo[:, t, s], F_hi[:, t, :])]
            accumulate("OUT_fc", g, bank, products)

        residual("fc", x2_bias, ["x2_bias", "rstd_lnf"], x3, lambda g: ["T_L2", "x3_bias"], rstd["lnf"])

        transposed("L2", x3, lambda g: "out_fc", "S_L2")

        @step("S_L2")
        def _(g):
            pe.wait("hi_L2", g)
            pe.wait("b2", g)
            bank = held["S_L2", g] = banks.take("exp_L2", g)
            for b in range(GROUP):
                s = slice(b * P, (b + 1) * P)
                for e in range(T):
                    pe.op(mm, bank[:, s], at(B2, g)[:, e, s], at(xT_hi["L2"], g)[:, e, s], start=e == 0, stop=e == T - 1,
                          done=("S_L2", g) if b == GROUP - 1 and e == T - 1 else None)

        softmax("L2", "O_L2", "prob_L2")

        @step("O_L2")
        def _(g):
            pe.wait("prob_L2", g)
            bank = held["O_L2", g] = banks.take("oT_lo_L2", g)
            p = at(prob["L2"], g)
            for b in range(GROUP):
                pe.op(mm, bank[:, b * P:(b + 1) * P], at(ctx_in, g)[:, b, :], p[:, b, :], start=True, stop=True)
            for b in range(GROUP):
                pe.op(mm, bank[:, TOK + b:TOK + b + 1], p[:, b, :], ones_col[:], start=True, stop=True,
                      done=("O_L2", g) if b == GROUP - 1 else None)

        @step("sums_L2")
        def _(g):
            act.wait("O_L2", g)
            act.wait("x3_bias", g - len(token_sums))
            act.op(nc.scalar.activation, at(token_sums, g)[:], held["O_L2", g][:, TOK:TOK + GROUP], ACT.Copy,
                   done=("sums_L2", g))

        split_evacuation("O_L2", "oT_hi_L2", "oT_lo_L2", oT_hi["L2"], oT_lo["L2"], "OUT_L2")

        @step("x3_bias")
        def _(g):
            dve.wait("bias", "L2v")
            dve.wait("out_fc", g)
            dve.wait("sums_L2", g)
            for b in range(GROUP):
                dve.op(v.scalar_tensor_tensor, out=at(x3_bias, g)[:, b, :], in0=bias["L2v"][:],
                        scalar=at(token_sums, g)[:, b:b + 1], in1=at(x3, g)[:, b, :], op0=ALU.mult, op1=ALU.add,
                        done=("x3_bias", g) if b == GROUP - 1 else None)

        project("L2", [("L2", Wv2_hi, Wv2_lo)])
        residual("L2", x3_bias, ["x3_bias"], x4, lambda g: ["norm_ln2"])
        moments("ln2", [x4], lambda g: ["out_L2"], EPS_L2, "shift_ln2", "norm_ln2")
        layernorm("ln2", [x4], lambda g: ["out_L2"], xhat["ln2"], ["T_L3", "x_res"])

        @step("x_res")
        def _(g):
            pool.wait("gamma_row")
            pool.wait("bias", "L3")
            pool.wait("norm_ln2", g)
            pool.wait("out_L3", g - len(x_res))

            def every(row):
                return row[:].unsqueeze(1).to_broadcast([P, GROUP, D])

            pool.op(nc.gpsimd.tensor_tensor, at(x_res, g)[:], at(xhat["ln2"], g)[:], every(gamma_row), ALU.mult,
                    done=("x_gamma", g))
            pool.wait("x_gamma", g)
            pool.op(nc.gpsimd.tensor_tensor, at(x_res, g)[:], at(x_res, g)[:], every(bias["L3"]), ALU.add,
                    done=("x_res", g))
        transposed("L3", xhat["ln2"], lambda g: "norm_ln2", "Q_L3")
        queries_and_scores("L3", ctxT, ctx_loaded)
        softmax("L3", "PT_L3", "out_L3")
        attended("L3", ctx_in, "exp_L3")
        project("L3", N_of("L3"))
        residual("L3", x_res, ["x_res", "inv_L3"], y, lambda g: [loaded("stored", y, g)], inv_total["L3"])

        @step("store")
        def _(g):
            sp.wait("out_L3", g)
            sp.dma(nc.sync.dma_start, seqs(out, g), at(y, g)[:], done=(loaded("stored", y, g), g))

        order = [(STARTS[name] + COMES[g], g, name) for name in steps for g in range(GROUPS)]
        order += [(PREPARATIONS[name], -1, name) for name in preparations]
        for _, g, name in sorted(order):
            if g < 0:
                preparations[name]()
            else:
                steps[name](g)
        for g in range(GROUPS - len(y), GROUPS):
            sp.wait(loaded("stored", y, g), g)

        block = stack.enter_context(nc.Block())
        block.tensor(pe.play)
        block.scalar(act.play)
        block.vector(dve.play)
        block.gpsimd(pool.play)
        block.sync(sp.play)


def layout(inputs):
    import numpy as np

    def name(a, what):
        layer, side = a[:2], a[2:]
        return f"{layer}_xattn_{side + '_' if side else ''}{what}"

    def grouped(a, axes):
        return a.reshape(GROUPS, GROUP, *a.shape[1:]).transpose(0, *axes).reshape(GROUPS, P, -1)

    x, ctx = inputs["x"], inputs["ctx_512"]
    arrays = {"x": np.concatenate([grouped(x, (2, 1, 3)), grouped(x.reshape(BATCH, P, T, P), (4, 3, 1, 2))], axis=2),
              "ctx": np.concatenate([grouped(ctx, (2, 1, 3)), grouped(ctx, (3, 1, 2))], axis=2),
              "side": grouped(inputs["fside_BxSxS_0"], (2, 1, 3))}
    for a in ATTENTIONS + ["L2"]:
        arrays[f"{a}_WqT"] = inputs[name(a, "Wq")].T
        arrays[f"{a}_WkT"] = inputs[name(a, "Wk")].T
        if a != "L2":
            arrays[f"{a}_WvT"] = inputs[name(a, "Wv")].T
            arrays[f"{a}_Wo"] = inputs[name(a, "Wo")]
    arrays["L2_Wv"] = inputs["L2_xattn_Wv"]
    arrays["fc_W"] = inputs["L1_xattn_fc_W"]
    vectors = {"fc_g": "L1_xattn_ln_g", "fc_b": "L1_xattn_ln_b", "fc_bias": "L1_xattn_fc_b", "L2_bk": "L2_xattn_bk",
               "L2_bv": "L2_xattn_bv", "L3_g1": "L2_xattn_gamma", "L3_b1": "L2_xattn_beta"}
    for a in ATTENTIONS:
        for b in ("bq", "bv", "bo"):
            vectors[f"{a}_{b}"] = name(a, b)
    for a in ("L1a", "L1v"):
        for n in (1, 2):
            vectors[f"{a}_g{n}"] = name(a, f"ln{n}_g")
            vectors[f"{a}_b{n}"] = name(a, f"ln{n}_b")

    def padded(n):
        vector = inputs[vectors[n]]
        return np.concatenate([vector, np.zeros(D - vector.shape[0], vector.dtype)])

    arrays["cols"] = np.stack([padded(n).reshape(T, P) for n in COLS]).transpose(2, 0, 1).reshape(P, len(COLS) * T)
    arrays["rows"] = np.stack([padded(n) for n in ROWS])
    return {n: np.ascontiguousarray(a) for n, a in arrays.items()}


def kernel(**inputs):
    import numpy as np
    import concourse.bacc as bacc
    from concourse.bass_utils import run_bass_kernel_spmd

    nc = bacc.Bacc("TRN2", target_bir_lowering=False, num_devices=1)
    arrays = layout({n: np.asarray(a) for n, a in inputs.items()})
    ins = {n: nc.dram_tensor(f"in_{n}", a.shape, mybir.dt.from_np(a.dtype), kind="ExternalInput").ap()
           for n, a in arrays.items()}
    out = nc.dram_tensor("out", (BATCH, P, D), F32, kind="ExternalOutput").ap()
    build(nc, ins, out)
    result = run_bass_kernel_spmd(nc, [{f"in_{n}": a for n, a in arrays.items()}], core_ids=[0])
    return result.results[0]["out"]
```
